# Optimizing a Trainium2 kernel written in Bass

```python
import numpy as np
import jax
import jax.numpy as jnp

def _softmax(x, axis=-1):
    return jax.nn.softmax(x, axis=axis)

def _gelu(x):
    return jax.nn.gelu(x, approximate=True)

def _silu(x):
    return jax.nn.silu(x)

def _sigmoid(x):
    return jax.nn.sigmoid(x)

def _layernorm(x, axis=-1, eps=1e-05):
    m = jnp.mean(x, axis=axis, keepdims=True)
    v = jnp.var(x, axis=axis, keepdims=True)
    return (x - m) / jnp.sqrt(v + eps)

def _scatter_add(tgt, idx, src, axis=0):
    return tgt.at[idx].add(src)

def _segment_sum(src, seg, n):
    return jax.ops.segment_sum(src, seg, n)
kernel_name = 'mk_seq_postln_d1_jaxref_r8_f0b19b'

def setup_inputs(seed: int=0):
    np.random.seed(seed)
    _w = jnp.asarray

    def _L0_attn_setup():
        import jax, jax.numpy as jnp
        import numpy as np
        D_MODEL = 256
        EXPAND = 2
        D_INNER = EXPAND * D_MODEL
        D_SSM = D_INNER
        D_STATE = 128
        NGROUPS = 1
        HEADDIM = 64
        NHEADS = D_SSM // HEADDIM
        D_CONV = 4
        CHUNK = 32
        CONV_DIM = D_SSM + 2 * NGROUPS * D_STATE
        D_IN_PROJ = 2 * D_INNER + 2 * NGROUPS * D_STATE + NHEADS
        EPS = 1e-05

        def silu(x):
            return x * jax.nn.sigmoid(x)

        def softplus(x):
            return jnp.log1p(jnp.exp(-jnp.abs(x))) + jnp.maximum(x, 0)

        def segsum(x):
            T = x.shape[-1]
            xe = jnp.broadcast_to(x[..., :, None], x.shape + (T,))
            mask_lo = jnp.tril(jnp.ones((T, T), dtype=bool), k=-1)
            xe = jnp.where(mask_lo, xe, 0.0)
            s = jnp.cumsum(xe, axis=-2)
            mask = jnp.tril(jnp.ones((T, T), dtype=bool), k=0)
            return jnp.where(mask, s, -jnp.inf)

        def ssd(x, A, B, C, chunk_size):
            b, s, h, p = x.shape
            c = s // chunk_size
            resh = lambda m: m.reshape((b, c, chunk_size) + m.shape[2:])
            x, A, B, C = (resh(x), resh(A), resh(B), resh(C))
            A = jnp.transpose(A, (0, 3, 1, 2))
            A_cumsum = jnp.cumsum(A, axis=-1)
            L = jnp.exp(segsum(A))
            Y_diag = jnp.einsum('bclhn,bcshn,bhcls,bcshp->bclhp', C, B, L, x)
            decay_states = jnp.exp(A_cumsum[..., -1:] - A_cumsum)
            states = jnp.einsum('bclhn,bhcl,bclhp->bchpn', B, decay_states, x)
            init = jnp.zeros_like(states[:, :1])
            states = jnp.concatenate([init, states], axis=1)
            A_last = jnp.pad(A_cumsum[:, :, :, -1], ((0, 0), (0, 0), (1, 0)))
            decay_chunk = jnp.exp(segsum(A_last))
            new_states = jnp.einsum('bhzc,bchpn->bzhpn', decay_chunk, states)
            states, final_state = (new_states[:, :-1], new_states[:, -1])
            state_decay_out = jnp.exp(A_cumsum)
            Y_off = jnp.einsum('bclhn,bchpn,bhcl->bclhp', C, states, state_decay_out)
            Y = (Y_diag + Y_off).reshape(b, s, h, p)
            return (Y, final_state)
        key = jax.random.key(seed)
        ks = jax.random.split(key, 8)
        u = jax.random.normal(ks[0], (2, 512, D_MODEL), dtype=jnp.float32)
        W_in = jax.random.normal(ks[1], (D_MODEL, D_IN_PROJ), dtype=jnp.float32) * D_MODEL ** (-0.5)
        conv_w = jax.random.uniform(ks[2], (D_CONV, CONV_DIM), dtype=jnp.float32, minval=-0.1, maxval=0.1)
        conv_b = jnp.zeros((CONV_DIM,), dtype=jnp.float32)
        dt = jnp.exp(jax.random.uniform(ks[3], (NHEADS,)) * (np.log(0.1) - np.log(0.001)) + np.log(0.001))
        dt = jnp.clip(dt, 0.0001)
        dt_bias = dt + jnp.log(jnp.expm1(dt))
        A_log = jnp.log(jax.random.uniform(ks[4], (NHEADS,), minval=1.0, maxval=16.0))
        D = jnp.ones((NHEADS,), dtype=jnp.float32)
        norm_scale = jnp.ones((D_SSM,), dtype=jnp.float32)
        W_out = jax.random.normal(ks[5], (D_INNER, D_MODEL), dtype=jnp.float32) * D_INNER ** (-0.5)
        return {'u': u, 'W_in': W_in, 'conv_w': conv_w, 'conv_b': conv_b, 'dt_bias': dt_bias, 'A_log': A_log, 'D': D, 'norm_scale': norm_scale, 'W_out': W_out}
    _L0_attn_in = _L0_attn_setup()

    def _L0_ffn_setup():
        import jax, jax.numpy as jnp
        import numpy as np
        BLOCK_SIZE = 32
        HIDDEN_SIZE = 256
        MLP_DIM = 2048
        NVFP4_LUT = jnp.array([0.0, 0.5, 1.0, 1.5, 2.0, 3.0, 4.0, 6.0, 0.0, -0.5, -1.0, -1.5, -2.0, -3.0, -4.0, -6.0], dtype=jnp.float32)

        def dequant_nvfp4(W_packed, scales, block=BLOCK_SIZE):
            N = W_packed.shape[0]
            low = W_packed & 15
            high = W_packed >> 4 & 15
            idx = jnp.stack([low, high], axis=-1).reshape(N, -1)
            vals = NVFP4_LUT[idx]
            K = vals.shape[1]
            vals = vals.reshape(N, K // block, block) * scales[:, :, None]
            return vals.reshape(N, K)
        key = jax.random.key(seed)
        ks = jax.random.split(key, 7)
        x = jax.random.normal(ks[0], (4, 32, HIDDEN_SIZE), dtype=jnp.float32)
        gate_W_packed = jax.random.randint(ks[1], (MLP_DIM, HIDDEN_SIZE // 2), 0, 32, dtype=jnp.int32)
        gate_scales = jax.random.uniform(ks[2], (MLP_DIM, HIDDEN_SIZE // BLOCK_SIZE), dtype=jnp.float32) * 0.1 + 0.001
        up_W_packed = jax.random.randint(ks[3], (MLP_DIM, HIDDEN_SIZE // 2), 0, 32, dtype=jnp.int32)
        up_scales = jax.random.uniform(ks[4], (MLP_DIM, HIDDEN_SIZE // BLOCK_SIZE), dtype=jnp.float32) * 0.1 + 0.001
        down_W_packed = jax.random.randint(ks[5], (HIDDEN_SIZE, MLP_DIM // 2), 0, 32, dtype=jnp.int32)
        down_scales = jax.random.uniform(ks[6], (HIDDEN_SIZE, MLP_DIM // BLOCK_SIZE), dtype=jnp.float32) * 0.1 + 0.001
        return {'x': x, 'gate_W_packed': gate_W_packed, 'gate_scales': gate_scales, 'up_W_packed': up_W_packed, 'up_scales': up_scales, 'down_W_packed': down_W_packed, 'down_scales': down_scales}
    _L0_ffn_in = _L0_ffn_setup()
    _d = {'L0_attn_u': _L0_attn_in['u'], 'L0_attn_W_in': _L0_attn_in['W_in'], 'L0_attn_conv_w': _L0_attn_in['conv_w'], 'L0_attn_conv_b': _L0_attn_in['conv_b'], 'L0_attn_dt_bias': _L0_attn_in['dt_bias'], 'L0_attn_A_log': _L0_attn_in['A_log'], 'L0_attn_D': _L0_attn_in['D'], 'L0_attn_norm_scale': _L0_attn_in['norm_scale'], 'L0_attn_W_out': _L0_attn_in['W_out'], 'L0_ffn_gate_W_packed': _L0_ffn_in['gate_W_packed'], 'L0_ffn_gate_scales': _L0_ffn_in['gate_scales'], 'L0_ffn_up_W_packed': _L0_ffn_in['up_W_packed'], 'L0_ffn_up_scales': _L0_ffn_in['up_scales'], 'L0_ffn_down_W_packed': _L0_ffn_in['down_W_packed'], 'L0_ffn_down_scales': _L0_ffn_in['down_scales']}
    _x0 = _d['L0_attn_u']
    _d['L0_attn_u'] = jax.random.normal(jax.random.fold_in(jax.random.key(seed), 1), (16, 256, 256), dtype=_x0.dtype)
    del _x0
    return _d

def reference(L0_attn_u, L0_attn_W_in, L0_attn_conv_w, L0_attn_conv_b, L0_attn_dt_bias, L0_attn_A_log, L0_attn_D, L0_attn_norm_scale, L0_attn_W_out, L0_ffn_gate_W_packed, L0_ffn_gate_scales, L0_ffn_up_W_packed, L0_ffn_up_scales, L0_ffn_down_W_packed, L0_ffn_down_scales):

    def _L0_attn_ref(u, W_in, conv_w, conv_b, dt_bias, A_log, D, norm_scale, W_out):
        import jax, jax.numpy as jnp
        import numpy as np
        D_MODEL = 256
        EXPAND = 2
        D_INNER = EXPAND * D_MODEL
        D_SSM = D_INNER
        D_STATE = 128
        NGROUPS = 1
        HEADDIM = 64
        NHEADS = D_SSM // HEADDIM
        D_CONV = 4
        CHUNK = 32
        CONV_DIM = D_SSM + 2 * NGROUPS * D_STATE
        D_IN_PROJ = 2 * D_INNER + 2 * NGROUPS * D_STATE + NHEADS
        EPS = 1e-05

        def silu(x):
            return x * jax.nn.sigmoid(x)

        def softplus(x):
            return jnp.log1p(jnp.exp(-jnp.abs(x))) + jnp.maximum(x, 0)

        def segsum(x):
            T = x.shape[-1]
            xe = jnp.broadcast_to(x[..., :, None], x.shape + (T,))
            mask_lo = jnp.tril(jnp.ones((T, T), dtype=bool), k=-1)
            xe = jnp.where(mask_lo, xe, 0.0)
            s = jnp.cumsum(xe, axis=-2)
            mask = jnp.tril(jnp.ones((T, T), dtype=bool), k=0)
            return jnp.where(mask, s, -jnp.inf)

        def ssd(x, A, B, C, chunk_size):
            b, s, h, p = x.shape
            c = s // chunk_size
            resh = lambda m: m.reshape((b, c, chunk_size) + m.shape[2:])
            x, A, B, C = (resh(x), resh(A), resh(B), resh(C))
            A = jnp.transpose(A, (0, 3, 1, 2))
            A_cumsum = jnp.cumsum(A, axis=-1)
            L = jnp.exp(segsum(A))
            Y_diag = jnp.einsum('bclhn,bcshn,bhcls,bcshp->bclhp', C, B, L, x)
            decay_states = jnp.exp(A_cumsum[..., -1:] - A_cumsum)
            states = jnp.einsum('bclhn,bhcl,bclhp->bchpn', B, decay_states, x)
            init = jnp.zeros_like(states[:, :1])
            states = jnp.concatenate([init, states], axis=1)
            A_last = jnp.pad(A_cumsum[:, :, :, -1], ((0, 0), (0, 0), (1, 0)))
            decay_chunk = jnp.exp(segsum(A_last))
            new_states = jnp.einsum('bhzc,bchpn->bzhpn', decay_chunk, states)
            states, final_state = (new_states[:, :-1], new_states[:, -1])
            state_decay_out = jnp.exp(A_cumsum)
            Y_off = jnp.einsum('bclhn,bchpn,bhcl->bclhp', C, states, state_decay_out)
            Y = (Y_diag + Y_off).reshape(b, s, h, p)
            return (Y, final_state)
        b, s, _ = u.shape
        zxbcdt = u @ W_in
        z, xBC, dt = jnp.split(zxbcdt, [D_INNER, D_INNER + D_SSM + 2 * NGROUPS * D_STATE], axis=-1)
        xp = jnp.pad(xBC, ((0, 0), (D_CONV - 1, 0), (0, 0)))
        conv = conv_b
        for i in range(D_CONV):
            conv = conv + xp[:, i:i + s, :] * conv_w[i]
        xBC = silu(conv)
        x, B, C = jnp.split(xBC, [D_SSM, D_SSM + NGROUPS * D_STATE], axis=-1)
        x = x.reshape(b, s, NHEADS, HEADDIM)
        dt = softplus(dt + dt_bias)
        A = -jnp.exp(A_log)
        Bh = jnp.broadcast_to(B[:, :, None, :], (b, s, NHEADS, D_STATE))
        Ch = jnp.broadcast_to(C[:, :, None, :], (b, s, NHEADS, D_STATE))
        y, _final = ssd(x * dt[..., None], A * dt, Bh, Ch, CHUNK)
        y = y + x * D[None, None, :, None]
        y = y.reshape(b, s, D_SSM)
        y = y * silu(z)
        var = jnp.mean(jnp.square(y), axis=-1, keepdims=True)
        y = y * jax.lax.rsqrt(var + EPS) * norm_scale
        return y @ W_out

    def _L0_ffn_ref(x, gate_W_packed, gate_scales, up_W_packed, up_scales, down_W_packed, down_scales):
        import jax, jax.numpy as jnp
        import numpy as np
        BLOCK_SIZE = 32
        HIDDEN_SIZE = 256
        MLP_DIM = 2048
        NVFP4_LUT = jnp.array([0.0, 0.5, 1.0, 1.5, 2.0, 3.0, 4.0, 6.0, 0.0, -0.5, -1.0, -1.5, -2.0, -3.0, -4.0, -6.0], dtype=jnp.float32)

        def dequant_nvfp4(W_packed, scales, block=BLOCK_SIZE):
            N = W_packed.shape[0]
            low = W_packed & 15
            high = W_packed >> 4 & 15
            idx = jnp.stack([low, high], axis=-1).reshape(N, -1)
            vals = NVFP4_LUT[idx]
            K = vals.shape[1]
            vals = vals.reshape(N, K // block, block) * scales[:, :, None]
            return vals.reshape(N, K)
        B, S, H = x.shape
        xt = x.reshape(B * S, H)
        Wg = dequant_nvfp4(gate_W_packed, gate_scales)
        Wu = dequant_nvfp4(up_W_packed, up_scales)
        Wd = dequant_nvfp4(down_W_packed, down_scales)
        gate = jnp.einsum('th,nh->tn', xt, Wg)
        up = jnp.einsum('th,nh->tn', xt, Wu)
        gelu = jnp.tanh(0.7978845608028654 * (gate + 0.044715 * gate ** 3)) * gate * 0.5 + gate * 0.5
        inter = gelu * up
        out = jnp.einsum('tn,hn->th', inter, Wd)
        return out.reshape(B, S, H)
    x = L0_attn_u
    x = _layernorm(x + _L0_attn_ref(x, L0_attn_W_in, L0_attn_conv_w, L0_attn_conv_b, L0_attn_dt_bias, L0_attn_A_log, L0_attn_D, L0_attn_norm_scale, L0_attn_W_out), axis=-1)
    x = _layernorm(x + _L0_ffn_ref(x, L0_ffn_gate_W_packed, L0_ffn_gate_scales, L0_ffn_up_W_packed, L0_ffn_up_scales, L0_ffn_down_W_packed, L0_ffn_down_scales), axis=-1)
    return x

_drawn_inputs = setup_inputs


def setup_inputs(seed=0):
    import zlib

    import numpy as np

    out = dict(_drawn_inputs(seed))
    spreads = {'L0_attn_conv_b': (0.0, 0.1), 'L0_attn_D': (1.0, 0.2), 'L0_attn_norm_scale': (1.0, 0.2)}
    factors = {}
    for name, (base, spread) in spreads.items():
        noise = np.random.default_rng([zlib.crc32(name.encode()), seed]).standard_normal(out[name].shape)
        drawn = base * np.exp(spread * noise) if base else spread * noise
        out[name] = jnp.asarray(drawn.astype(out[name].dtype))
    for name, factor in factors.items():
        out[name] = (out[name] * factor).astype(out[name].dtype)
    return out
```

```python
from contextlib import ExitStack

import concourse.bass as bass
from concourse import mybir

ALU = mybir.AluOpType
ACT = mybir.ActivationFunctionType
F32 = mybir.dt.float32
F32R = mybir.dt.float32r
I32 = mybir.dt.int32
U16 = mybir.dt.uint16
BF16 = mybir.dt.bfloat16

P = 128
EPS = 1e-5
QUARTER_BITS = 124 << 7

USES = (["uT0", "uT1", "dt", "x4", "x5", "x0", "x1", "x2", "x3", "z0", "z1", "z2", "z3", "CB0", "XT0",
         "D0a", "D0b", "Y0", "XT1", "D1a", "D1b", "Y1", "Yoff0", "CB1", "gT0", "XT2", "D2a", "D2b",
         "op0", "gT1", "Y2", "XT3", "D3a", "D3b", "op1", "gT2", "Y3", "Yoff1", "op2", "gT3", "op3"])
CONV_ORDER = (4, 5, 0, 1, 2, 3)
SLOTS = [["uT"], ["dt", "x4", "x5"], ["x0", "x1"], ["x2", "x3"], ["z0", "z1"], ["z2", "z3"],
         ["CB0", "R0", "XT0"], ["D0"], ["R1", "Y0", "XT1"], ["D1"], ["R2", "Y1", "CB1", "gT0", "XT2"], ["D2"],
         ["R3", "op0", "gT1", "Y2", "XT3"], ["D3"], ["op1", "gT2", "Y3"], ["op2", "gT3"], ["op3", "ln1"]]


def stages(rest, slots=len(SLOTS)):
    order, at = [], 0
    for n, slot in enumerate(SLOTS):
        order += [(name, None) for name in slot]
        upto = min((n + 1) * len(rest) // slots, len(rest))
        order += [(None, r) for r in rest[at:upto]]
        at = upto
    return order


class Signal:

    def __init__(self, sem, per, base=0, step=1):
        self.sem, self.per, self.base, self.step = sem, per, base, step

    def at(self, group, k):
        return group * (self.per * self.step) + (self.base + k) * self.step


def wait(eng, signal, group, k):
    value = signal.at(group, k)
    if not isinstance(value, int) or value > 0:
        eng.wait_ge(signal.sem, value)


def mamba_ffn_kernel(nc, u, W_in, conv_w, conv_b, dt_bias, A_log, D, norm_scale, W_out,
                     gate_p, gate_s, up_p, up_s, down_p, down_s, out):
    BATCH, SEQ, DM = u.shape
    DI = norm_scale.shape[0]
    H = D.shape[0]
    HP = DI // H
    NIN = W_in.shape[1]
    FF = gate_p.shape[0]
    TOK = 512
    NT = TOK // P
    GROUPS = BATCH * SEQ // TOK
    KT = DM // P
    JT = DI // P
    CT = (NIN - H - DI) // P
    NF = FF // P
    UNITS = 12
    X0, DT0 = DI, NIN - H
    assert (SEQ, TOK // SEQ, KT, JT, CT, NF) == (256, 2, 2, 4, 6, 16)

    u_v = u.rearrange("b s d -> (b s) d").rearrange("(g t p) d -> g p t d", t=NT, p=P)
    out_v = out.rearrange("b s d -> (b s) d").rearrange("(g t p) d -> g p t d", t=NT, p=P)

    with ExitStack() as ctx:
        def sb(name, shape, dt=F32):
            return ctx.enter_context(nc.sbuf_tensor(name, shape, dt))

        def sig(name, per, base=0, step=1):
            return Signal(ctx.enter_context(nc.semaphore(name)), per, base, step)

        win_hi, win_lo = sb("win_hi", [P, KT, NIN], F32R), sb("win_lo", [P, KT, NIN], F32R)
        wout_hi, wout_lo = sb("wout_hi", [P, JT, DM], F32R), sb("wout_lo", [P, JT, DM], F32R)
        wg_hi, wg_lo = sb("wg_hi", [P, KT, FF], F32R), sb("wg_lo", [P, KT, FF], F32R)
        wu_hi, wu_lo = sb("wu_hi", [P, KT, FF], F32R), sb("wu_lo", [P, KT, FF], F32R)
        wd_hi, wd_lo = sb("wd_hi", [P, NF, DM], F32R), sb("wd_lo", [P, NF, DM], F32R)
        ident = sb("ident", [P, P])
        tri = sb("tri", [P, P])
        tri_r = sb("tri_r", [P, P], F32R)
        after_r = sb("after_r", [P, P], F32R)
        chan = sb("chan", [P, 34])
        dtb, a_neg, d_bc = sb("dtb", [P, H]), sb("a_neg", [P, H]), sb("d_bc", [P, H])
        half, eps, inv_di = sb("minus_half", [P, NT]), sb("eps", [P, NT]), sb("inv_di", [P, 1])
        g_sc, u_sc = sb("g_sc", [P, NF * 8]), sb("u_sc", [P, NF * 8])
        d_sc = sb("d_sc", [P, 2, 64])
        u_sb = sb("u_sb", [P, NT, DM])
        uT_hi, uT_lo = sb("uT_hi", [P, KT, TOK], F32R), sb("uT_lo", [P, KT, TOK], F32R)
        R_hi = uT_hi[:, :, :].rearrange("p k (h l) -> p (k h) l", l=P)
        R_lo = uT_lo[:, :, :].rearrange("p k (h l) -> p (k h) l", l=P)
        xbc = sb("xbc", [P, CT, TOK])
        zs = sb("zs", [P, NT, DI])
        dtx, dta, dte = sb("dtx", [P, NT * H]), sb("dta", [P, NT * H]), sb("dte", [P, NT * H])
        dts, dtq, dtp = sb("dts", [P, NT * H]), sb("dtq", [P, NT * H]), sb("dtp", [P, NT * H])
        dt_sb, dA = sb("dt_sb", [P, NT, H]), sb("dA", [P, NT, H])
        dA_hi, dA_lo = sb("dA_hi", [P, NT, H], F32R), sb("dA_lo", [P, NT, H], F32R)
        dec = sb("dec", [P, H, P])
        cb = sb("cb", [P, 3, P])
        e2 = sb("e2", [P, 2, H])
        xdt, xtail = sb("xdt", [P, DI]), sb("xtail", [P, DI])
        y = sb("y", [P, 2, DI])
        ssq, ms, rms_v, rms = (sb(name, [P, NT]) for name in ("ssq", "mean_square", "rms_v", "rms"))
        gT_hi, gT_lo = sb("gT_hi", [P, DI], F32R), sb("gT_lo", [P, DI], F32R)
        bn6, mv = sb("bn6", [P, NT, 6]), sb("mv", [P, NT, 2])
        lnv, lnr = sb("lnv", [P, NT]), sb("lnr", [P, NT])
        h_sb = sb("h_sb", [P, NT, DM])
        h_res = sb("h_res", [P, NT, DM])
        hT_hi, hT_lo = sb("hT_hi", [P, KT, TOK], F32R), sb("hT_lo", [P, KT, TOK], F32R)
        act_sb = sb("act_sb", [P, 2, TOK])
        in_hi, in_lo = sb("in_hi", [P, 2, TOK], F32R), sb("in_lo", [P, 2, TOK], F32R)
        fbn6, fmv = sb("fbn6", [P, NT, 6]), sb("fmv", [P, NT, 2])
        flnv, flnr = sb("flnv", [P, NT]), sb("flnr", [P, NT])
        win_raw = xbc[:, :, :].rearrange("p c t -> p (c t)")[:, 0:KT * NIN].rearrange("p (k n) -> p k n", k=KT)
        wout_raw = zs[:, 0:2, :].rearrange("p a (b d) -> p (a b) d", d=DM)
        rows = y[0:34, 0, 0:P]
        raw = h_res[:, :, :].rearrange("p (b a) d -> p b (a d)", b=2).bitcast(I32)
        raw16 = h_res[:, :, :].bitcast(U16).rearrange("p (b a) (d w) -> p b (a d) w", b=2, w=2)[:, :, :, 0]
        code = act_sb[:, 0, :].bitcast(U16).rearrange("p (a j) -> p a j", a=2)
        other = act_sb[:, 1, :].bitcast(U16).rearrange("p (a j) -> p a j", a=2)
        wdq = h_sb[:, :, :].rearrange("p (a b) d -> p a (b d)", a=2)

        MB = [ctx.enter_context(nc.psum_tensor(f"mixer{b}", [P, 512], F32)) for b in range(4)]
        GB = ctx.enter_context(nc.psum_tensor("gate_bank", [P, 512], F32))
        UB = ctx.enter_context(nc.psum_tensor("up_bank", [P, 512], F32))
        OB = [ctx.enter_context(nc.psum_tensor(f"down{b}", [P, 512], F32)) for b in range(2)]

        per_bank = [len(USES[b::4]) for b in range(4)]
        bank_ready = [sig(f"mixer{b}_ready", per_bank[b], base=1 if b == 0 else 0) for b in range(4)]
        const_in = sig("const_in", 0, step=16)
        win_in, wout_in = sig("win_in", 0, step=16), sig("wout_in", 0, step=16)
        codes_in = [sig(f"codes_in{b}", 0, step=16) for b in range(2)]
        consts = sig("consts", 0)
        crt = sig("consts_rounded", 0)
        a_exp = sig("a_exp", 0)
        win_ok, wout_ok = sig("win_split", 0), sig("wout_split", 0)
        win_top, wout_top = sig("win_hi_done", 0), sig("wout_hi_done", 0)
        wsc = sig("wout_scaled", 0)
        cstep = sig("code_step", 0)
        quad = sig("scales_times_four", 0)
        deq = sig("dequantized", 0)
        wt_hi = sig("weights_hi", 0)
        wt_lo = sig("weights_lo", 0)
        u_in = sig("u_in", 1, step=16)
        uT_h, uT_l = sig("uT_hi_done", 2), sig("uT_lo_done", 2)
        dt_abs, dt_exp, dt_step = sig("dt_abs", 1), sig("dt_exp", 1), sig("dt_step", 18)
        dA_ok = sig("dA_split", 1)
        conv0, conv = sig("conv_first_tap", 6), sig("conv_taps", 18)
        xbc_ok, zs_ok = sig("xbc_ready", 6), sig("zs_ready", 4)
        R_ok, dec_ok, W_ok = sig("R_ready", 4), sig("decay_ready", 8), sig("W_ready", 4)
        cb_act, cb_ok = sig("cb_scalar_part", 2), sig("cb_ready", 2)
        x_ok, xt_ok = sig("xdt_ready", 4), sig("xtail_ready", 2)
        y_step = sig("y_step", 16)
        ssq_ok, rms_step = sig("ssq_ready", 4), sig("rms_step", 12)
        gT_h, gT_l = sig("gT_hi_done", 4), sig("gT_lo_done", 4)
        r_ok, ln_bn, ln_mv, ln_pow, h_ok = (sig("residual", 4), sig("ln_stats", 4), sig("ln_mean_var", 4),
                                            sig("ln_pow", 2), sig("h_ready", 4))
        G_ready, U_ready = sig("gate_ready", 17, UNITS), sig("up_ready", 17, UNITS)
        hres_ok = sig("h_res_ready", 1, step=16)
        hT_h, hT_l = sig("hT_hi_done", 2), sig("hT_lo_done", 2)
        gelu_ok, inter_ok = sig("gelu_ready", 16), sig("inter_ready", 16)
        in_h, in_l, down_ok = sig("inter_hi", 16), sig("inter_lo", 16), sig("down_done", 16)
        o_sum, o_bn, o_mv, o_pow, o_ok = (sig("out_residual", 4), sig("out_stats", 4), sig("out_mean_var", 4),
                                          sig("out_pow", 2), sig("out_ready", 4))
        stored = sig("stored", 1, step=16)

        def bank(use):
            return MB[USES.index(use) % 4]

        def ready(use):
            n = USES.index(use)
            return bank_ready[n % 4], n // 4 + 1

        def wait_ready(eng, use, g):
            s, k = ready(use)
            wait(eng, s, g, k)

        read_by = {"uT0": (uT_l, 1), "uT1": (uT_l, 2), "dt": (dt_step, 1)}
        for n, c in enumerate(CONV_ORDER):
            read_by[f"x{c}"] = (conv, 3 * n + 3)
        for q in range(2):
            read_by[f"CB{q}"], read_by[f"Yoff{q}"] = (cb_ok, q + 1), (y_step, 8 * q + 6)
        for t in range(4):
            read_by |= {f"z{t}": (zs_ok, t + 1), f"XT{t}": (x_ok, t + 1), f"D{t}a": (dec_ok, 2 * t + 1),
                        f"D{t}b": (dec_ok, 2 * t + 2), f"Y{t}": (y_step, (2, 5, 10, 13)[t]),
                        f"gT{t}": (gT_l, t + 1), f"op{t}": (r_ok, t + 1)}

        def wait_bank(eng, use, g):
            n = USES.index(use)
            if n >= 4:
                s, k = read_by[USES[n - 4]]
                wait(eng, s, g, k)
            else:
                s, k = read_by[USES[n::4][-1]]
                wait(eng, s, g - 1, k)

        def f32(ap):
            return ap.bitcast(F32)

        ffn_items = [("F1", 0)] + [("unit", n) for n in range(NF)] + [("down", NF - 1), ("final", 0)]
        prep_items = [("prep", n) for n in range(UNITS)]

        def prep_dst(n, a):
            kind, i = n // 4, n % 4
            if kind < 2:
                return [w[:, a, i * 512:(i + 1) * 512].rearrange("p (q m) -> p q m", q=4)
                        for w in ((wg_hi, wg_lo), (wu_hi, wu_lo))[kind]]
            t0 = 8 * (i % 2) + a
            return [w[:, t0:t0 + 7:2, (i // 2) * P:(i // 2 + 1) * P] for w in (wd_hi, wd_lo)]

        block = ctx.enter_context(nc.Block())

        @block.sync
        def _(sp):
            sp.dma_start(rows[0:24, :], conv_w.rearrange("i (c p) -> (i c) p", p=P)).then_inc(const_in.sem, 16)
            sp.dma_start(rows[24:30, :], conv_b.rearrange("(c p) -> c p", p=P)).then_inc(const_in.sem, 16)
            sp.dma_start(rows[30:34, :], norm_scale.rearrange("(c p) -> c p", p=P)).then_inc(const_in.sem, 16)
            sp.dma_start(dtb[:, :], dt_bias.partition_broadcast(P)).then_inc(const_in.sem, 16)
            sp.dma_start(a_neg[:, :], A_log.partition_broadcast(P)).then_inc(const_in.sem, 16)
            sp.dma_start(d_bc[:, :], D.partition_broadcast(P)).then_inc(const_in.sem, 16)
            sp.dma_start(u_sb[:, :, :], u_v[0]).then_inc(u_in.sem, 16)
            sp.dma_start(win_raw, W_in.rearrange("(k p) n -> p k n", p=P)).then_inc(win_in.sem, 16)
            for sc, src in ((g_sc, gate_s), (u_sc, up_s)):
                sp.dma_start(sc[:, :].rearrange("p (b c) -> p b c", b=NF // 2),
                             src.rearrange("(b p a) c -> p b (a c)", p=P, a=2)).then_inc(const_in.sem, 16)
            sp.dma_start(d_sc[:, :, :], down_s.rearrange("(t p) b -> p t b", p=P)).then_inc(const_in.sem, 16)

            def load_codes(n):
                if n >= 2:
                    wait(sp, cstep, 0, 8 * (n - 1))
                kind, i = n // 4, n % 4
                if kind < 2:
                    src = (gate_p, up_p)[kind].rearrange("(b p a) j -> p b (a j)", p=P, a=2)[:, 2 * i:2 * i + 2, :]
                    dst = raw[:, n % 2, :].rearrange("p (b j) -> p b j", b=2)
                else:
                    src = down_p.rearrange("(t p) j -> p t j", p=P)[:, i // 2, (i % 2) * 512:(i % 2) * 512 + 512]
                    dst = raw[:, n % 2, :]
                sp.dma_start(dst, src).then_inc(codes_in[n % 2].sem, 16)

            load_codes(0)
            load_codes(1)
            sp.dma_start(wout_raw, W_out.rearrange("(j p) d -> p j d", p=P)).then_inc(wout_in.sem, 16)
            for n in range(2, UNITS):
                load_codes(n)

            def wait_for(*rises):
                values = [s.at(g, k) for s, g, k in rises]
                values = [v if isinstance(v, int) else sp.to_reg(v) for v in values]
                sp.wait_ge(win_in.sem, 16)
                for (s, _, _), v in zip(rises, values):
                    sp.wait_ge(s.sem, v)

            def load_u(g):
                wait_for((r_ok, g - 1, 4))
                sp.dma_start(u_sb[:, :, :], u_v[g]).then_inc(u_in.sem, 16)

            def store(f):
                wait_for((o_ok, f, 4))
                sp.dma_start(out_v[f], h_res[:, :, :]).then_inc(stored.sem, 16)

            def keep_h(f):
                wait_for((h_ok, f, 4), *([(stored, f, 0)] if not isinstance(f, int) or f > 0 else []))
                sp.dma_start(h_res[:, :, :], h_sb[:, :, :]).then_inc(hres_ok.sem, 16)

            load_u(1)
            keep_h(0)
            with sp.Fori(1, GROUPS - 1) as g:
                load_u(g + 1)
                store(g - 1)
                keep_h(g)
            store(GROUPS - 2)
            keep_h(GROUPS - 1)
            store(GROUPS - 1)
            wait(sp, stored, GROUPS - 1, 1)

        @block.tensor
        def _(pe):
            def mm3(dst, left, right, first, last):
                (lh, ll), (rh, rl) = left, right
                nc.tensor.matmul(dst, lh, rh, start=first, stop=False, skip_group_check=True)
                nc.tensor.matmul(dst, lh, rl, start=False, stop=False, skip_group_check=True)
                return nc.tensor.matmul(dst, ll, rh, start=False, stop=last, skip_group_check=True)

            def mixer(name, g):
                kind, i = name.rstrip("0123456789"), name[-1]
                i = int(i) if i.isdigit() else 0
                if kind == "uT":
                    wait(pe, u_in, g, 1)
                    for k in range(KT):
                        use = f"uT{k}"
                        wait_bank(pe, use, g)
                        for t in range(NT):
                            mm = nc.tensor.transpose(bank(use)[:, t * P:(t + 1) * P],
                                                     u_sb[:, t, k * P:(k + 1) * P], ident[:, :])
                        mm.then_inc(ready(use)[0].sem, 1)
                elif kind == "dt":
                    wait_bank(pe, "dt", g)
                    wait(pe, uT_l, g, 2)
                    for t in range(NT):
                        for k in range(KT):
                            mm = mm3(bank("dt")[:, t * H:(t + 1) * H],
                                     [x[:, k, t * P:(t + 1) * P] for x in (uT_hi, uT_lo)],
                                     [w[:, k, DT0:NIN] for w in (win_hi, win_lo)], k == 0, k == KT - 1)
                    mm.then_inc(ready("dt")[0].sem, 1)
                elif kind == "x":
                    use, c0 = f"x{i}", X0 + i * P
                    wait_bank(pe, use, g)
                    for k in range(KT):
                        mm = mm3(bank(use)[:, :], [w[:, k, c0:c0 + P] for w in (win_hi, win_lo)],
                                 [x[:, k, :] for x in (uT_hi, uT_lo)], k == 0, k == KT - 1)
                    mm.then_inc(ready(use)[0].sem, 1)
                elif kind == "z":
                    use = f"z{i}"
                    wait_bank(pe, use, g)
                    for k in range(KT):
                        mm = mm3(bank(use)[:, :], [x[:, k, i * P:(i + 1) * P] for x in (uT_hi, uT_lo)],
                                 [w[:, k, 0:DI] for w in (win_hi, win_lo)], k == 0, k == KT - 1)
                    mm.then_inc(ready(use)[0].sem, 1)
                elif kind == "CB":
                    use, s = f"CB{i}", i * SEQ
                    wait_bank(pe, use, g)
                    wait(pe, xbc_ok, g, 6)
                    wait(pe, dA_ok, g, 1)
                    b = bank(use)
                    nc.tensor.matmul(b[:, 0:2 * P], xbc[:, 4, s:s + P], xbc[:, 5, s:s + 2 * P],
                                     start=True, stop=True)
                    nc.tensor.matmul(b[:, 2 * P:3 * P], xbc[:, 4, s + P:s + 2 * P], xbc[:, 5, s + P:s + 2 * P],
                                     start=True, stop=True)
                    nc.tensor.matmul(b[:, 3 * P:3 * P + H], tri_r[:, :], dA_hi[:, 2 * i + 1, :],
                                     start=True, stop=False)
                    nc.tensor.matmul(b[:, 3 * P:3 * P + H], tri_r[:, :], dA_lo[:, 2 * i + 1, :],
                                     start=False, stop=True).then_inc(ready(use)[0].sem, 1)
                elif kind == "XT":
                    use = f"XT{i}"
                    wait_bank(pe, use, g)
                    for j in range(JT):
                        mm = nc.tensor.transpose(bank(use)[:, j * P:(j + 1) * P],
                                                 xbc[:, j, i * P:(i + 1) * P], ident[:, :])
                    mm.then_inc(ready(use)[0].sem, 1)
                elif kind == "D":
                    wait(pe, R_ok, g, i + 1)
                    for n, use in enumerate((f"D{i}a", f"D{i}b")):
                        wait_bank(pe, use, g)
                        hs = slice(4 * n, 4 * n + 4)
                        nc.tensor.matmul(bank(use)[:, :], after_r[:, :], R_hi[:, hs, :], start=True, stop=False)
                        nc.tensor.matmul(bank(use)[:, :], after_r[:, :], R_lo[:, hs, :], start=False,
                                         stop=True).then_inc(ready(use)[0].sem, 1)
                elif kind == "Y":
                    use = f"Y{i}"
                    wait_bank(pe, use, g)
                    wait(pe, x_ok, g, i + 1)
                    wait(pe, W_ok, g, i + 1)
                    for h in range(H):
                        mm = nc.tensor.matmul(bank(use)[:, h * HP:(h + 1) * HP], dec[:, h, :],
                                              xdt[:, h * HP:(h + 1) * HP], start=True, stop=True)
                    mm.then_inc(ready(use)[0].sem, 1)
                    if i % 2:
                        use = f"Yoff{i // 2}"
                        wait_bank(pe, use, g)
                        wait(pe, xt_ok, g, i // 2 + 1)
                        nc.tensor.matmul(bank(use)[:, :], cb[:, 1, :], xtail[:, :], start=True,
                                         stop=True).then_inc(ready(use)[0].sem, 1)
                elif kind == "gT":
                    use = f"gT{i}"
                    wait_bank(pe, use, g)
                    wait(pe, y_step, g, (3, 8, 11, 16)[i])
                    for j in range(JT):
                        mm = nc.tensor.transpose(bank(use)[:, j * P:(j + 1) * P],
                                                 zs[:, i, j * P:(j + 1) * P], ident[:, :])
                    mm.then_inc(ready(use)[0].sem, 1)
                elif kind == "op":
                    use = f"op{i}"
                    wait_bank(pe, use, g)
                    wait(pe, gT_l, g, i + 1)
                    for j in range(JT):
                        mm = mm3(bank(use)[:, 0:DM], [x[:, j * P:(j + 1) * P] for x in (gT_hi, gT_lo)],
                                 [w[:, j, :] for w in (wout_hi, wout_lo)], j == 0, j == JT - 1)
                    mm.then_inc(ready(use)[0].sem, 1)

            def down(n, f):
                wait(pe, in_l, f, n + 1)
                for t in range(NT):
                    mm = mm3(OB[t // 2][:, (t % 2) * DM:(t % 2 + 1) * DM],
                             [x[:, n % 2, t * P:(t + 1) * P] for x in (in_hi, in_lo)],
                             [w[:, n, :] for w in (wd_hi, wd_lo)], n == 0 and t % 2 == 0, n == NF - 1)
                mm.then_inc(down_ok.sem, 1)

            def ffn(kind, n, f):
                if kind == "F1":
                    wait(pe, h_ok, f, 4)
                    for k, (b, done) in enumerate(((GB, G_ready), (UB, U_ready))):
                        for t in range(NT):
                            mm = nc.tensor.transpose(b[:, t * P:(t + 1) * P], h_sb[:, t, k::2], ident[:, :])
                        mm.then_inc(done.sem, 1)
                elif kind == "unit":
                    if n == 0:
                        wait(pe, hT_l, f, 2)
                    for wh, wl, b, done, read in ((wg_hi, wg_lo, GB, G_ready, gelu_ok),
                                                  (wu_hi, wu_lo, UB, U_ready, inter_ok)):
                        if n:
                            wait(pe, read, f, n)
                        for k in range(KT):
                            mm = mm3(b[:, :], [w[:, k, n * P:(n + 1) * P] for w in (wh, wl)],
                                     [x[:, k, :] for x in (hT_hi, hT_lo)], k == 0, k == KT - 1)
                        mm.then_inc(done.sem, 1)
                    if n:
                        down(n - 1, f)
                elif kind == "down":
                    down(n, f)

            def prep(n):
                wait(pe, deq, 0, 2 * n + 2)
                for a, (b, done) in enumerate(((GB, G_ready), (UB, U_ready))):
                    if n:
                        pe.wait_ge(wt_lo.sem, 2 * n - 1 + a)
                    for q in range(4):
                        mm = nc.tensor.transpose(b[:, q * P:(q + 1) * P], wdq[:, a, q * P:(q + 1) * P], ident[:, :])
                    mm.then_inc(done.sem, 1)

            pe.wait_ge(consts.sem, 5)
            pe.wait_ge(const_in.sem, 16 * 9)
            nc.tensor.transpose(MB[0][:, 0:34], rows, ident[0:34, 0:34]).then_inc(bank_ready[0].sem, 1)
            pe.wait_ge(crt.sem, 3)
            for name, item in stages(prep_items, 12):
                if name:
                    if name == "dt":
                        pe.wait_ge(win_ok.sem, 2)
                    if name == "CB0":
                        pe.wait_ge(crt.sem, 4)
                    if name == "op0":
                        pe.wait_ge(wout_ok.sem, 1)
                    if name[0] != "R":
                        mixer(name, 0)
                else:
                    prep(item[1])
            pe.wait_ge(wt_lo.sem, 2 * UNITS)
            with pe.Fori(1, GROUPS) as g:
                for name, item in stages(ffn_items):
                    if name:
                        if name[0] != "R":
                            mixer(name, g)
                    else:
                        ffn(*item, g - 1)
            for item in ffn_items:
                ffn(*item, GROUPS - 1)

        @block.scalar
        def _(act):
            def silu(n, g):
                c = CONV_ORDER[n]
                wait(act, conv, g, 3 * n + 3)
                nc.scalar.activation(xbc[:, c, :], xbc[:, c, :], ACT.Silu).then_inc(xbc_ok.sem, 1)

            def mixer(name, g):
                kind, i = name.rstrip("0123456789"), name[-1]
                i = int(i) if i.isdigit() else 0
                if kind == "uT":
                    wait_ready(act, "D3b", g - 1)
                    for k in range(KT):
                        wait_ready(act, f"uT{k}", g)
                        nc.scalar.activation(uT_hi[:, k, :], bank(f"uT{k}")[:, :], ACT.Copy).then_inc(uT_h.sem, 1)
                elif kind == "dt":
                    wait(act, dt_abs, g, 1)
                    nc.scalar.activation(dte[:, :], dta[:, :], ACT.Exp, scale=-1.0).then_inc(dt_exp.sem, 1)
                elif kind == "x":
                    n = CONV_ORDER.index(i)
                    wait_ready(act, f"x{i}", g)
                    wait_ready(act, "XT3", g - 1)
                    nc.scalar.activation(xbc[:, i, :], bank(f"x{i}")[:, :], ACT.Identity,
                                         bias=chan[:, 24 + i:25 + i],
                                         scale=chan[:, 18 + i:19 + i]).then_inc(conv0.sem, 1)
                    if n:
                        silu(n - 1, g)
                elif kind == "z":
                    if i == 0:
                        silu(CT - 1, g)
                    wait_ready(act, f"z{i}", g)
                    wait_ready(act, f"gT{i}", g - 1)
                    wait(act, ssq_ok, g - 1, i + 1)
                    nc.scalar.activation(zs[:, i, :], bank(f"z{i}")[:, :], ACT.Silu).then_inc(zs_ok.sem, 1)
                elif kind == "CB":
                    wait_ready(act, f"CB{i}", g)
                    if i:
                        wait_ready(act, "Yoff0", g)
                    else:
                        wait_ready(act, "Yoff1", g - 1)
                    nc.scalar.activation(cb[:, 1, :], bank(f"CB{i}")[:, P:2 * P], ACT.Copy)
                    nc.scalar.activation(e2[:, i, :], bank(f"CB{i}")[:, 3 * P:3 * P + H],
                                         ACT.Exp).then_inc(cb_act.sem, 1)
                elif kind == "D":
                    if i:
                        wait_ready(act, f"Y{i - 1}", g)
                    else:
                        wait_ready(act, "Y3", g - 1)
                    for n, use in enumerate((f"D{i}a", f"D{i}b")):
                        wait_ready(act, use, g)
                        nc.scalar.activation(dec[:, 4 * n:4 * n + 4, :],
                                             bank(use)[:, :].rearrange("p (h l) -> p h l", h=4),
                                             ACT.Exp).then_inc(dec_ok.sem, 1)
                elif kind == "gT":
                    wait(act, y_step, g, (3, 8, 11, 16)[i])
                    nc.scalar.activation(y[:, i % 2, :], zs[:, i, :], ACT.Square,
                                         accum_out=ssq[:, i:i + 1]).then_inc(ssq_ok.sem, 1)
                    wait_ready(act, f"gT{i}", g)
                    if i:
                        wait_ready(act, f"op{i - 1}", g)
                    else:
                        wait_ready(act, "op3", g - 1)
                    nc.scalar.activation(gT_hi[:, :], bank(f"gT{i}")[:, :], ACT.Copy).then_inc(gT_h.sem, 1)

            def inter_hi(n, f):
                wait(act, inter_ok, f, n + 1)
                if n >= 2:
                    wait(act, down_ok, f, n - 1)
                nc.scalar.activation(in_hi[:, n % 2, :], act_sb[:, n % 2, :], ACT.Copy).then_inc(in_h.sem, 1)

            def ffn(kind, n, f):
                if kind == "F1":
                    for k, (b, done) in enumerate(((GB, G_ready), (UB, U_ready))):
                        wait(act, done, f, 1)
                        nc.scalar.activation(hT_hi[:, k, :], b[:, :], ACT.Copy).then_inc(hT_h.sem, 1)
                elif kind == "unit":
                    if n:
                        inter_hi(n - 1, f)
                    wait(act, G_ready, f, n + 2)
                    if n >= 2:
                        wait(act, in_l, f, n - 1)
                    nc.scalar.activation(act_sb[:, n % 2, :], GB[:, :], ACT.Gelu_apprx_tanh).then_inc(gelu_ok.sem, 1)
                elif kind == "down":
                    inter_hi(n, f)

            def prep(n):
                for a, (b, done) in enumerate(((GB, G_ready), (UB, U_ready))):
                    act.wait_ge(done.sem, n + 1)
                    dst, _ = prep_dst(n, a)
                    nc.scalar.activation(dst, b[:, :].rearrange("p (q m) -> p q m", q=4),
                                         ACT.Copy).then_inc(wt_hi.sem, 1)

            act.wait_ge(const_in.sem, 16 * 9)
            nc.scalar.activation(a_neg[:, :], a_neg[:, :], ACT.Exp).then_inc(a_exp.sem, 1)
            act.wait_ge(win_in.sem, 16)
            for k in range(KT):
                nc.scalar.activation(win_hi[:, k, :], win_raw[:, k, :], ACT.Copy).then_inc(win_top.sem, 1)
            act.wait_ge(wsc.sem, 4)
            nc.scalar.activation(wout_hi[:, :, :], wout_raw, ACT.Copy).then_inc(wout_top.sem, 1)
            for name, item in stages(prep_items, 12):
                if name:
                    if name == "x4":
                        act.wait_ge(crt.sem, 4)
                        act.wait_ge(win_ok.sem, 2)
                    if name == "z0":
                        act.wait_ge(wout_ok.sem, 1)
                    mixer(name, 0)
                else:
                    prep(item[1])
            with act.Fori(1, GROUPS) as g:
                for name, item in stages(ffn_items):
                    if name:
                        mixer(name, g)
                    else:
                        ffn(*item, g - 1)
            for item in ffn_items:
                ffn(*item, GROUPS - 1)

        @block.vector
        def _(dve):
            tt, ts, stt = nc.vector.tensor_tensor, nc.vector.tensor_scalar, nc.vector.scalar_tensor_tensor

            def head(ap):
                return ap.rearrange("p (h c) -> p h c", h=H)

            def mixer(name, g):
                kind, i = name.rstrip("0123456789"), name[-1]
                i = int(i) if i.isdigit() else 0
                if kind == "uT":
                    for k in range(KT):
                        wait(dve, uT_h, g, k + 1)
                        tt(uT_lo[:, k, :], bank(f"uT{k}")[:, :], f32(uT_hi[:, k, :]), ALU.subtract)\
                            .then_inc(uT_l.sem, 1)
                elif kind == "dt":
                    n = [0]

                    def link(ins):
                        n[0] += 1
                        ins.then_inc(dt_step.sem, 1)
                        wait(dve, dt_step, g, n[0])

                    wait_ready(dve, "dt", g)
                    link(tt(dtx[:, :].rearrange("p (t h) -> p t h", t=NT),
                            bank("dt")[:, 0:NT * H].rearrange("p (t h) -> p t h", t=NT),
                            dtb[:, :].unsqueeze(1).to_broadcast([P, NT, H]), ALU.add))
                    stt(dta[:, :], dtx[:, :], -1.0, dtx[:, :], ALU.mult, ALU.max).then_inc(dt_abs.sem, 1)
                    wait(dve, dt_exp, g, 1)
                    link(ts(dtp[:, :], dte[:, :], 2.0, None, ALU.add))
                    link(nc.vector.reciprocal(dtp[:, :], dtp[:, :]))
                    link(tt(dts[:, :], dte[:, :], dtp[:, :], ALU.mult))
                    link(tt(dtq[:, :], dts[:, :], dts[:, :], ALU.mult))
                    link(ts(dtp[:, :], dtq[:, :], 1.0 / 17, None, ALU.mult))
                    for odd in (15, 13, 11, 9, 7, 5, 3):
                        link(stt(dtp[:, :], dtp[:, :], 1.0 / odd, dtq[:, :], ALU.add, ALU.mult))
                    link(stt(dtp[:, :], dtp[:, :], 1.0, dts[:, :], ALU.add, ALU.mult))
                    link(ts(dtx[:, :], dtx[:, :], 0.0, None, ALU.max))
                    flat = dt_sb[:, :, :].rearrange("p t h -> p (t h)")
                    link(stt(flat, dtp[:, :], 2.0, dtx[:, :], ALU.mult, ALU.add))
                    link(tt(dA[:, :, :], dt_sb[:, :, :], a_neg[:, :].unsqueeze(1).to_broadcast([P, NT, H]),
                            ALU.mult))
                    link(nc.vector.tensor_copy(dA_hi[:, :, :], dA[:, :, :]))
                    assert n[0] == 18, n
                    tt(dA_lo[:, :, :], dA[:, :, :], f32(dA_hi[:, :, :]), ALU.subtract).then_inc(dA_ok.sem, 1)
                elif kind == "x":
                    n = CONV_ORDER.index(i)
                    acc = xbc[:, i, :].rearrange("p (q s) -> p q s", q=2)
                    src = bank(f"x{i}")[:, :].rearrange("p (q s) -> p q s", q=2)
                    wait(dve, conv0, g, n + 1)
                    for d in (1, 2, 3):
                        c = (3 - d) * CT + i
                        ins = stt(acc[:, :, d:], src[:, :, 0:SEQ - d], chan[:, c:c + 1], acc[:, :, d:],
                                  ALU.mult, ALU.add)
                        ins.then_inc(conv.sem, 1)
                        wait(dve, conv, g, 3 * n + d)
                elif kind == "CB":
                    wait(dve, cb_act, g, i + 1)
                    tt(cb[:, 0, :], bank(f"CB{i}")[:, 0:P], tri[:, :], ALU.mult)
                    tt(cb[:, 2, :], bank(f"CB{i}")[:, 2 * P:3 * P], tri[:, :], ALU.mult).then_inc(cb_ok.sem, 1)
                elif kind == "XT":
                    use = f"XT{i}"
                    wait_ready(dve, use, g)
                    wait(dve, ssq_ok, g, i - 1)
                    tt(head(y[:, i % 2, :]), head(bank(use)[:, :]),
                       d_bc[:, :].unsqueeze(2).to_broadcast([P, H, HP]), ALU.mult).then_inc(y_step.sem, 1)
                    tt(head(xdt[:, :]), head(bank(use)[:, :]),
                       dt_sb[:, i, :].unsqueeze(2).to_broadcast([P, H, HP]), ALU.mult).then_inc(x_ok.sem, 1)
                elif kind == "D":
                    wait(dve, dec_ok, g, 2 * i + 2)
                    if i % 2 == 0:
                        wait(dve, x_ok, g, i + 1)
                        tt(head(xtail[:, :]), head(xdt[:, :]), dec[:, :, P - 1:P].to_broadcast([P, H, HP]),
                           ALU.mult).then_inc(xt_ok.sem, 1)
                        wait(dve, xt_ok, g, i // 2 + 1)
                    wait(dve, cb_ok, g, i // 2 + 1)
                    tt(dec[:, :, :], dec[:, :, :], cb[:, 2 * (i % 2):2 * (i % 2) + 1, :].to_broadcast([P, H, P]),
                       ALU.mult).then_inc(W_ok.sem, 1)
                elif kind == "Y":
                    s0 = (0, 3, 8, 11)[i]
                    yc = y[:, i % 2, :]
                    wait_ready(dve, f"Y{i}", g)
                    wait(dve, y_step, g, s0 + 1)
                    tt(yc, bank(f"Y{i}")[:, :], yc, ALU.add).then_inc(y_step.sem, 1)
                    wait(dve, y_step, g, s0 + 2)
                    s0 += 2
                    if i % 2:
                        use = f"Yoff{i // 2}"
                        wait_ready(dve, use, g)
                        tt(head(xdt[:, :]), head(bank(use)[:, :]),
                           e2[:, i // 2, :].unsqueeze(2).to_broadcast([P, H, HP]), ALU.mult)\
                            .then_inc(y_step.sem, 1)
                        wait(dve, y_step, g, s0 + 1)
                        tt(yc, yc, xdt[:, :], ALU.add).then_inc(y_step.sem, 1)
                        wait(dve, y_step, g, s0 + 2)
                    wait(dve, zs_ok, g, i + 1)
                    tt(zs[:, i, :], zs[:, i, :], yc, ALU.mult).then_inc(y_step.sem, 1)
                elif kind == "gT":
                    wait(dve, gT_h, g, i + 1)
                    tt(gT_lo[:, :], bank(f"gT{i}")[:, :], f32(gT_hi[:, :]), ALU.subtract).then_inc(gT_l.sem, 1)
                elif kind == "op":
                    if i == 0:
                        wait(dve, hres_ok, g, 0)
                    wait_ready(dve, f"op{i}", g)
                    wait(dve, rms_step, g, 3 * i + 3)
                    stt(h_sb[:, i, :], bank(f"op{i}")[:, 0:DM], rms[:, i:i + 1], u_sb[:, i, :],
                        ALU.mult, ALU.add).then_inc(r_ok.sem, 1)
                elif kind == "ln":
                    norm(h_sb, bn6, mv, lnr, (r_ok, ln_bn, ln_mv, ln_pow, h_ok), g)

            def norm(x, six, two, rs, signals, g):
                summed, stats, moments, power, done = signals
                for t in range(NT):
                    wait(dve, summed, g, t + 1)
                    nc.vector.bn_stats(six[:, t, :], x[:, t, :]).then_inc(stats.sem, 1)
                for t in range(NT):
                    dve.wait_ge(consts.sem, 5)
                    wait(dve, stats, g, t + 1)
                    nc.vector.bn_aggr(two[:, t, :], six[:, t, :]).then_inc(moments.sem, 1)
                wait(dve, moments, g, 4)
                wait(dve, power, g, 2)
                for t in range(NT):
                    ts(x[:, t, :], x[:, t, :], two[:, t, 0:1], rs[:, t:t + 1], ALU.subtract, ALU.mult)\
                        .then_inc(done.sem, 1)

            def inter_lo(n, f):
                wait(dve, in_h, f, n + 1)
                tt(in_lo[:, n % 2, :], act_sb[:, n % 2, :], f32(in_hi[:, n % 2, :]), ALU.subtract)\
                    .then_inc(in_l.sem, 1)

            def ffn(kind, n, f):
                if kind == "F1":
                    for k, b in enumerate((GB, UB)):
                        wait(dve, hT_h, f, k + 1)
                        tt(hT_lo[:, k, :], b[:, :], f32(hT_hi[:, k, :]), ALU.subtract).then_inc(hT_l.sem, 1)
                elif kind == "unit":
                    if n:
                        inter_lo(n - 1, f)
                    wait(dve, gelu_ok, f, n + 1)
                    wait(dve, U_ready, f, n + 2)
                    tt(act_sb[:, n % 2, :], UB[:, :], act_sb[:, n % 2, :], ALU.mult).then_inc(inter_ok.sem, 1)
                elif kind == "down":
                    inter_lo(n, f)
                elif kind == "final":
                    wait(dve, down_ok, f, NF)
                    wait(dve, hres_ok, f, 1)
                    for t in range(NT):
                        tt(h_res[:, t, :], OB[t // 2][:, (t % 2) * DM:(t % 2 + 1) * DM], h_res[:, t, :],
                           ALU.add).then_inc(o_sum.sem, 1)
                    norm(h_res, fbn6, fmv, flnr, (o_sum, o_bn, o_mv, o_pow, o_ok), f)

            def prep(n):
                src = raw16[:, n % 2, :]
                c2 = code.rearrange("p a j -> p (a j)")
                o2 = other.rearrange("p a j -> p (a j)")
                s0 = 8 * n
                dve.wait_ge(codes_in[n % 2].sem, 16 * (n // 2 + 1))
                if n:
                    wait(dve, deq, 0, 2 * n)
                ts(code[:, 0, :], src, 7, 6, ALU.bitwise_and, ALU.logical_shift_left).then_inc(cstep.sem, 1)
                ts(code[:, 1, :], src, 0x70, 2, ALU.bitwise_and, ALU.logical_shift_left).then_inc(cstep.sem, 1)
                wait(dve, cstep, 0, s0 + 2)
                ts(c2, c2, QUARTER_BITS, None, ALU.bitwise_or).then_inc(cstep.sem, 1)
                wait(dve, cstep, 0, s0 + 3)
                ts(o2.bitcast(BF16), c2.bitcast(BF16), 2.0, -0.25, ALU.mult, ALU.add).then_inc(cstep.sem, 1)
                wait(dve, cstep, 0, s0 + 4)
                tt(c2.bitcast(BF16), c2.bitcast(BF16), o2.bitcast(BF16), ALU.min).then_inc(cstep.sem, 1)
                wait(dve, cstep, 0, s0 + 5)
                ts(other[:, 0, :], src, 8, 12, ALU.bitwise_and, ALU.logical_shift_left).then_inc(cstep.sem, 1)
                ts(other[:, 1, :], src, 0x80, 8, ALU.bitwise_and, ALU.logical_shift_left).then_inc(cstep.sem, 1)
                wait(dve, cstep, 0, s0 + 7)
                tt(c2, c2, o2, ALU.bitwise_or).then_inc(cstep.sem, 1)
                for a, b in enumerate((GB, UB)):
                    dve.wait_ge(wt_hi.sem, 2 * n + a + 1)
                    hi, lo = prep_dst(n, a)
                    tt(lo, b[:, :].rearrange("p (q m) -> p q m", q=4), f32(hi), ALU.subtract)\
                        .then_inc(wt_lo.sem, 1)

            dve.wait_ge(consts.sem, 5)
            nc.vector.tensor_copy(tri_r[:, :], tri[:, :]).then_inc(crt.sem, 1)
            ts(after_r[:, :], tri[:, :], -1.0, 1.0, ALU.mult, ALU.add).then_inc(crt.sem, 1)
            dve.wait_ge(bank_ready[0].sem, 1)
            nc.vector.tensor_copy(chan[:, :], MB[0][:, 0:34]).then_inc(crt.sem, 1)
            dve.wait_ge(crt.sem, 3)
            dve.wait_ge(a_exp.sem, 1)
            ts(a_neg[:, :], a_neg[:, :], -1.0, None, ALU.mult).then_inc(crt.sem, 1)
            dve.wait_ge(wout_in.sem, 16)
            for j in range(JT):
                ts(wout_raw[:, j, :], wout_raw[:, j, :], chan[:, 30 + j:31 + j], None, ALU.mult)\
                    .then_inc(wsc.sem, 1)
            for k in range(KT):
                dve.wait_ge(win_top.sem, k + 1)
                tt(win_lo[:, k, :], win_raw[:, k, :], f32(win_hi[:, k, :]), ALU.subtract).then_inc(win_ok.sem, 1)
            dve.wait_ge(wout_top.sem, 1)
            tt(wout_lo[:, :, :], wout_raw, f32(wout_hi[:, :, :]), ALU.subtract).then_inc(wout_ok.sem, 1)
            for name, item in stages(prep_items, 12):
                if name:
                    if name == "op0":
                        wait(dve, U_ready, -1, 17)
                    mixer(name, 0)
                else:
                    prep(item[1])
            with dve.Fori(1, GROUPS) as g:
                for name, item in stages(ffn_items):
                    if name:
                        mixer(name, g)
                    else:
                        ffn(*item, g - 1)
            for item in ffn_items:
                ffn(*item, GROUPS - 1)

        @block.gpsimd
        def _(pool):
            tt, ts = nc.gpsimd.tensor_tensor, nc.gpsimd.tensor_scalar

            def rsqrt(dst, tmp, var, signal, g, k, n):
                tt(tmp, var, eps[:, 0:n], ALU.add).then_inc(signal.sem, 1)
                wait(pool, signal, g, k)
                tt(dst, tmp, half[:, 0:n], ALU.pow).then_inc(signal.sem, 1)

            def mixer(name, g):
                kind, i = name.rstrip("0123456789"), name[-1]
                i = int(i) if i.isdigit() else 0
                if kind == "R":
                    if i:
                        wait_ready(pool, f"D{i - 1}b", g)
                    else:
                        wait_ready(pool, "z3", g)
                    wait(pool, dA_ok, g, 1)
                    mask = tri[:, :].unsqueeze(1).to_broadcast([P, H, P])
                    for R, step in ((R_hi, dA_hi), (R_lo, dA_lo)):
                        ins = tt(R, mask, f32(step[:, i, :]).unsqueeze(2).to_broadcast([P, H, P]), ALU.mult)
                    ins.then_inc(R_ok.sem, 1)
                elif kind == "gT":
                    wait(pool, ssq_ok, g, i + 1)
                    tt(ms[:, i:i + 1], ssq[:, i:i + 1], inv_di[:, :], ALU.mult).then_inc(rms_step.sem, 1)
                    wait(pool, rms_step, g, 3 * i + 1)
                    rsqrt(rms[:, i:i + 1], rms_v[:, i:i + 1], ms[:, i:i + 1], rms_step, g, 3 * i + 2, 1)
                elif kind == "ln":
                    wait(pool, ln_mv, g, 4)
                    rsqrt(lnr[:, :], lnv[:, :], mv[:, :, 1], ln_pow, g, 1, NT)

            def ffn(kind, n, f):
                if kind == "final":
                    wait(pool, o_mv, f, 4)
                    rsqrt(flnr[:, :], flnv[:, :], fmv[:, :, 1], o_pow, f, 1, NT)

            def prep(n):
                sc = (g_sc[:, (n % 4) * 32:(n % 4 + 1) * 32], u_sc[:, (n % 4) * 32:(n % 4 + 1) * 32],
                      d_sc[:, (n % 4) // 2, (n % 2) * 32:(n % 2 + 1) * 32])[n // 4]
                wait(pool, cstep, 0, 8 * n + 8)
                if n:
                    pool.wait_ge(U_ready.sem, n)
                for a in range(2):
                    tt(wdq[:, a, :].rearrange("p (b k) -> p b k", b=32),
                       code[:, a, :].bitcast(BF16).rearrange("p (b k) -> p b k", b=32),
                       sc.unsqueeze(2).to_broadcast([P, 32, 16]), ALU.mult).then_inc(deq.sem, 1)

            nc.gpsimd.memset(ident[:, :], 0.0).then_inc(consts.sem, 1)
            nc.gpsimd.memset(tri[:, :], 1.0).then_inc(consts.sem, 1)
            nc.gpsimd.memset(half[:, :], -0.5)
            nc.gpsimd.memset(eps[:, :], EPS)
            nc.gpsimd.memset(inv_di[:, :], 1.0 / DI).then_inc(consts.sem, 1)
            pool.wait_ge(consts.sem, 3)
            nc.gpsimd.affine_select(out=ident[:, :], in_=ident[:, :], compare_op=ALU.not_equal, fill=1.0, base=0,
                                    pattern=[[-1, P]], channel_multiplier=1).then_inc(consts.sem, 1)
            nc.gpsimd.affine_select(out=tri[:, :], in_=tri[:, :], compare_op=ALU.is_ge, fill=0.0, base=0,
                                    pattern=[[1, P]], channel_multiplier=-1).then_inc(consts.sem, 1)
            pool.wait_ge(consts.sem, 5)
            pool.wait_ge(const_in.sem, 16 * 9)
            for sc in (g_sc[:, :], u_sc[:, :], d_sc[:, :, :]):
                ts(sc, sc, 4.0, None, ALU.mult).then_inc(quad.sem, 1)
            pool.wait_ge(quad.sem, 3)
            for name, item in stages(prep_items, 12):
                if name:
                    mixer(name, 0)
                else:
                    prep(item[1])
            with pool.Fori(1, GROUPS) as g:
                for name, item in stages(ffn_items):
                    if name:
                        mixer(name, g)
                    else:
                        ffn(*item, g - 1)
            for item in ffn_items:
                ffn(*item, GROUPS - 1)


_INS = ["L0_attn_u", "L0_attn_W_in", "L0_attn_conv_w", "L0_attn_conv_b", "L0_attn_dt_bias", "L0_attn_A_log",
        "L0_attn_D", "L0_attn_norm_scale", "L0_attn_W_out", "L0_ffn_gate_W_packed", "L0_ffn_gate_scales",
        "L0_ffn_up_W_packed", "L0_ffn_up_scales", "L0_ffn_down_W_packed", "L0_ffn_down_scales"]
_OUTS = [((16, 256, 256), "float32")]


def kernel(**inputs):
    import numpy as _np
    import concourse.bacc as _bacc
    from concourse import mybir as _mybir
    from concourse.bass_utils import run_bass_kernel_spmd as _run

    nc = _bacc.Bacc("TRN2", target_bir_lowering=False, num_devices=1)
    arrays, args = {}, []
    for name in _INS:
        a = _np.ascontiguousarray(inputs[name])
        arrays[f"in_{name}_dram"] = a
        args.append(nc.dram_tensor(f"in_{name}_dram", a.shape, _mybir.dt.from_np(a.dtype), kind="ExternalInput").ap())
    for i, (shape, dtype) in enumerate(_OUTS):
        dt = _mybir.dt.from_np(_np.dtype(dtype))
        args.append(nc.dram_tensor(f"out_{i}_dram", shape, dt, kind="ExternalOutput").ap())
    mamba_ffn_kernel(nc, *args)
    r = _run(nc, [arrays], core_ids=[0])
    got = tuple(r.results[0][f"out_{i}_dram"] for i in range(len(_OUTS)))
    return got[0]
```

```python
from contextlib import ExitStack

import concourse.bass as bass
from concourse import mybir

ALU = mybir.AluOpType
ACT = mybir.ActivationFunctionType
F32 = mybir.dt.float32
F32R = mybir.dt.float32r
I32 = mybir.dt.int32
U16 = mybir.dt.uint16
BF16 = mybir.dt.bfloat16

P = 128
EPS = 1e-5
QUARTER_BITS = 124 << 7

USES = (["uT0", "uT1", "dt", "x4", "x5", "x0", "x1", "x2", "x3", "z0", "z1", "z2", "z3", "CB0", "XT0",
         "D0a", "D0b", "Y0", "XT1", "D1a", "D1b", "Y1", "Yoff0", "CB1", "gT0", "XT2", "D2a", "D2b",
         "op0", "gT1", "Y2", "XT3", "D3a", "D3b", "op1", "gT2", "Y3", "Yoff1", "op2", "gT3", "op3"])
CONV_ORDER = (4, 5, 0, 1, 2, 3)
SLOTS = [["dt", "x4", "x5"], ["x0", "x1"], ["x2", "x3"], ["z0", "z1"], ["z2", "z3"], ["CB0", "R0", "XT0"],
         ["D0"], ["R1", "Y0", "XT1"], ["D1"], ["R2", "Y1", "CB1", "gT0", "XT2"], ["D2"],
         ["R3", "op0", "gT1", "Y2", "XT3"], ["D3"], ["op1", "gT2", "Y3"], ["op2", "gT3"], ["op3", "ln1"]]


BEFORE_H = [n for n, slot in enumerate(SLOTS) if "op0" in slot][0]


def stages(kind, units, slots):
    order, at = [], 0
    for n, slot in enumerate(SLOTS):
        order += [("mixer", name) for name in slot]
        upto = min((n + 1) * len(units) // slots, len(units))
        order += [(kind, r) for r in units[at:upto]]
        at = upto
    return order


def split_name(name):
    kind = name.rstrip("0123456789")
    return kind, int(name[len(kind):] or 0)


class Signal:

    def __init__(self, sem, per, base=0, step=1):
        self.sem, self.per, self.base, self.step = sem, per, base, step

    def at(self, group, k):
        return group * (self.per * self.step) + (self.base + k) * self.step


def wait(eng, signal, group, k):
    value = signal.at(group, k)
    if not isinstance(value, int) or value > 0:
        eng.wait_ge(signal.sem, value)


def mamba_ffn_kernel(nc, u, W_in, conv_w, conv_b, dt_bias, A_log, D, norm_scale, W_out,
                     gate_p, gate_s, up_p, up_s, down_p, down_s, out):
    BATCH, SEQ, DM = u.shape
    DI = norm_scale.shape[0]
    H = D.shape[0]
    HP = DI // H
    NIN = W_in.shape[1]
    FF = gate_p.shape[0]
    TOK = 512
    NT = TOK // P
    GROUPS = BATCH * SEQ // TOK
    KT = DM // P
    JT = DI // P
    CT = (NIN - H - DI) // P
    NF = FF // P
    UNITS = 12
    X0, DT0 = DI, NIN - H
    assert (SEQ, TOK // SEQ, KT, JT, CT, NF) == (256, 2, 2, 4, 6, 16)

    u_v = u.rearrange("b s d -> (b s) d").rearrange("(g t p) d -> g p t d", t=NT, p=P)
    out_v = out.rearrange("b s d -> (b s) d").rearrange("(g t p) d -> g p t d", t=NT, p=P)

    with ExitStack() as ctx:
        def sb(name, shape, dt=F32):
            return ctx.enter_context(nc.sbuf_tensor(name, shape, dt))

        def sig(name, per, base=0, step=1):
            return Signal(ctx.enter_context(nc.semaphore(name)), per, base, step)

        win_hi, win_lo = sb("win_hi", [P, KT, NIN], F32R), sb("win_lo", [P, KT, NIN], F32R)
        wout_hi, wout_lo = sb("wout_hi", [P, JT, DM], F32R), sb("wout_lo", [P, JT, DM], F32R)
        wg_hi, wg_lo = sb("wg_hi", [P, KT, FF], F32R), sb("wg_lo", [P, KT, FF], F32R)
        wu_hi, wu_lo = sb("wu_hi", [P, KT, FF], F32R), sb("wu_lo", [P, KT, FF], F32R)
        wd_hi, wd_lo = sb("wd_hi", [P, NF, DM], F32R), sb("wd_lo", [P, NF, DM], F32R)
        ident = sb("ident", [P, P])
        tri = sb("tri", [P, P])
        tri_r = sb("tri_r", [P, P], F32R)
        minus_ident_r = sb("minus_ident_r", [P, P], F32R)
        after_r = sb("after_r", [P, P], F32R)
        chan = sb("chan", [P, 34])
        dtb, a_neg, d_bc = sb("dtb", [P, H]), sb("a_neg", [P, H]), sb("d_bc", [P, H])
        half, eps, inv_di = sb("minus_half", [P, NT]), sb("eps", [P, NT]), sb("inv_di", [P, 1])
        eps4 = sb("eps4", [P, 1])
        g_sc, u_sc = sb("g_sc", [P, NF * 8]), sb("u_sc", [P, NF * 8])
        d_sc = sb("d_sc", [P, 2, 64])
        u_sb = sb("u_sb", [P, NT, DM])
        uT_hi, uT_lo = sb("uT_hi", [P, KT, TOK], F32R), sb("uT_lo", [P, KT, TOK], F32R)
        R_hi = uT_hi[:, :, :].rearrange("p k (h l) -> p (k h) l", l=P)
        R_lo = uT_lo[:, :, :].rearrange("p k (h l) -> p (k h) l", l=P)
        xbc = sb("xbc", [P, CT, TOK])
        zs = sb("zs", [P, NT, DI])
        dtx, dta, dte = sb("dtx", [P, NT * H]), sb("dta", [P, NT * H]), sb("dte", [P, NT * H])
        dts, dtq, dtp = sb("dts", [P, NT * H]), sb("dtq", [P, NT * H]), sb("dtp", [P, NT * H])
        dt_sb, dA = sb("dt_sb", [P, NT, H]), sb("dA", [P, NT, H])
        dA_hi, dA_lo = sb("dA_hi", [P, NT, H], F32R), sb("dA_lo", [P, NT, H], F32R)
        dec = sb("dec", [P, H, P])
        cb = sb("cb", [P, 3, P])
        e2 = sb("e2", [P, 2, H])
        xdt, xtail = sb("xdt", [P, DI]), sb("xtail", [P, DI])
        y = sb("y", [P, 2, DI])
        ssq, ms, rms_v, rms = (sb(name, [P, NT]) for name in ("ssq", "mean_square", "rms_v", "rms"))
        gT_hi, gT_lo = sb("gT_hi", [P, DI], F32R), sb("gT_lo", [P, DI], F32R)
        bn6, mv = sb("bn6", [P, NT, 6]), sb("mv", [P, NT, 2])
        lnv, lnr = sb("lnv", [P, NT]), sb("lnr", [P, NT])
        h_sb = sb("h_sb", [P, NT, DM])
        h_res = sb("h_res", [P, NT, DM])
        hT_hi, hT_lo = sb("hT_hi", [P, KT, TOK], F32R), sb("hT_lo", [P, KT, TOK], F32R)
        act_sb = sb("act_sb", [P, 2, TOK])
        in_hi, in_lo = sb("in_hi", [P, 2, TOK], F32R), sb("in_lo", [P, 2, TOK], F32R)
        fbn6, fmv = sb("fbn6", [P, NT, 6]), sb("fmv", [P, NT, 2])
        flnv, flnr = sb("flnv", [P, NT]), sb("flnr", [P, NT])
        win_raw = xbc[:, :, :].rearrange("p c t -> p (c t)")[:, 0:KT * NIN].rearrange("p (k n) -> p k n", k=KT)
        wout_raw = zs[:, 0:2, :].rearrange("p a (b d) -> p (a b) d", d=DM)
        rows = y[0:34, 0, 0:P]
        raw = h_res[:, :, :].rearrange("p (b a) d -> p b (a d)", b=2).bitcast(I32)
        raw16 = h_res[:, :, :].bitcast(U16).rearrange("p (b a) (d w) -> p b (a d) w", b=2, w=2)[:, :, :, 0]
        code = act_sb[:, 0, :].bitcast(U16).rearrange("p (a j) -> p a j", a=2)
        other = act_sb[:, 1, :].bitcast(U16).rearrange("p (a j) -> p a j", a=2)
        wdq = h_sb[:, :, :].rearrange("p (a b) d -> p a (b d)", a=2)

        MB = [ctx.enter_context(nc.psum_tensor(f"mixer{b}", [P, 512], F32)) for b in range(4)]
        GB = ctx.enter_context(nc.psum_tensor("gate_bank", [P, 512], F32))
        UB = ctx.enter_context(nc.psum_tensor("up_bank", [P, 512], F32))
        OB = [ctx.enter_context(nc.psum_tensor(f"down{b}", [P, 512], F32)) for b in range(2)]

        per_bank = [len(USES[b::4]) for b in range(4)]
        bank_ready = [sig(f"mixer{b}_ready", per_bank[b], base=1 if b == 0 else 0) for b in range(4)]
        rows_in = sig("rows_in", 0, step=16)
        small_in = sig("small_in", 0, step=16)
        gsc_in, sc_in = sig("gate_scales_in", 0, step=16), sig("scales_in", 0, step=16)
        win_in, wout_in = sig("win_in", 0, step=16), sig("wout_in", 0, step=16)
        codes_in = [sig(f"codes_in{b}", 0, step=16) for b in range(2)]
        consts = sig("consts", 0)
        crt = sig("consts_rounded", 0)
        a_exp, a_ready = sig("a_exp", 0), sig("a_ready", 0)
        win_ok, wout_ok = sig("win_split", 0), sig("wout_split", 0)
        win_top, wout_top = sig("win_hi_done", 0), sig("wout_hi_done", 0)
        wsc = sig("wout_scaled", 0)
        cstep = sig("code_step", 0)
        quad = sig("scales_times_four", 0)
        deq = sig("dequantized", 0)
        wt_hi = sig("weights_hi", 0)
        wt_lo = sig("weights_lo", 0)
        u_in = sig("u_in", 1, step=16)
        uT_h, uT_l = sig("uT_hi_done", 2), sig("uT_lo_done", 2)
        dt_exp, dt_step = sig("dt_exp", 1), sig("dt_step", 19)
        dA_ok = sig("dA_split", 1)
        conv0, conv = sig("conv_first_tap", 6), sig("conv_taps", 18)
        x_tanh, z_tanh = sig("x_tanh", 6), sig("z_tanh", 4)
        xbc_ok, zs_ok = sig("xbc_ready", 6), sig("zs_ready", 4)
        R_ok, dec_ok, W_ok = sig("R_ready", 4), sig("decay_ready", 8), sig("W_ready", 4)
        cb_act, cb_ok = sig("cb_scalar_part", 2), sig("cb_ready", 2)
        x_ok, xt_ok = sig("xdt_ready", 4), sig("xtail_ready", 2)
        y_step = sig("y_step", 16)
        ssq_ok, rms_step = sig("ssq_ready", 4), sig("rms_step", 12)
        gT_h, gT_l = sig("gT_hi_done", 4), sig("gT_lo_done", 4)
        r_ok, ln_bn, ln_mv, ln_pow, h_ok = (sig("residual", 4), sig("ln_stats", 4), sig("ln_mean_var", 4),
                                            sig("ln_pow", 2), sig("h_ready", 4))
        G_ready, U_ready = sig("gate_ready", 17, 2 * UNITS), sig("up_ready", 17, 2 * UNITS)
        hres_ok = sig("h_res_ready", 1, step=16)
        hT_h, hT_l = sig("hT_hi_done", 2), sig("hT_lo_done", 2)
        gelu_ok, inter_ok = sig("gelu_ready", 16), sig("inter_ready", 16)
        in_h, in_l, down_ok = sig("inter_hi", 16), sig("inter_lo", 16), sig("down_done", 16)
        o_sum, o_bn, o_mv, o_pow, o_ok = (sig("out_residual", 4), sig("out_stats", 4), sig("out_mean_var", 4),
                                          sig("out_pow", 2), sig("out_ready", 4))
        stored = sig("stored", 1, step=16)

        def bank(use):
            return MB[USES.index(use) % 4]

        def ready(use):
            n = USES.index(use)
            return bank_ready[n % 4], n // 4 + 1

        def wait_ready(eng, use, g):
            s, k = ready(use)
            wait(eng, s, g, k)

        read_by = {"uT0": (uT_l, 1), "uT1": (uT_l, 2), "dt": (dt_step, 1)}
        for n, c in enumerate(CONV_ORDER):
            read_by[f"x{c}"] = (conv, 3 * n + 3)
        for q in range(2):
            read_by[f"CB{q}"], read_by[f"Yoff{q}"] = (cb_ok, q + 1), (y_step, 8 * q + 6)
        for t in range(4):
            read_by |= {f"z{t}": (zs_ok, t + 1), f"XT{t}": (x_ok, t + 1), f"D{t}a": (dec_ok, 2 * t + 1),
                        f"D{t}b": (dec_ok, 2 * t + 2), f"Y{t}": (y_step, (2, 5, 10, 13)[t]),
                        f"gT{t}": (gT_l, t + 1), f"op{t}": (r_ok, t + 1)}

        def wait_bank(eng, use, g):
            n = USES.index(use)
            if n >= 4:
                s, k = read_by[USES[n - 4]]
                wait(eng, s, g, k)
            else:
                s, k = read_by[USES[n::4][-1]]
                wait(eng, s, g - 1, k)

        def f32(ap):
            return ap.bitcast(F32)

        def run(g, last, mixer, ffn, prep=None):
            if prep:
                order = stages("prep", range(1, UNITS + 1), BEFORE_H)
            else:
                order = stages("unit", range(NF), len(SLOTS))
            for kind, item in order:
                if kind == "mixer":
                    mixer(item, g)
                elif kind == "prep":
                    prep(item)
                else:
                    ffn(kind, item, g - 1)
            if not last:
                mixer("uT", g + 1)
            if not prep:
                ffn("down", NF - 2, g - 1)
            ffn("F1", 0, g)
            if not prep:
                ffn("down", NF - 1, g - 1)
                ffn("final", 0, g - 1)

        def run_end(ffn):
            for n in range(NF):
                ffn("unit", n, GROUPS - 1)
            for n in (NF - 2, NF - 1):
                ffn("down", n, GROUPS - 1)
            ffn("final", 0, GROUPS - 1)

        def prep_dst(n, a):
            kind, i = n // 4, n % 4
            if kind < 2:
                return [w[:, a, i * 512:(i + 1) * 512].rearrange("p (q m) -> p q m", q=4)
                        for w in ((wg_hi, wg_lo), (wu_hi, wu_lo))[kind]]
            t0 = 8 * (i % 2) + a
            return [w[:, t0:t0 + 7:2, (i // 2) * P:(i // 2 + 1) * P] for w in (wd_hi, wd_lo)]

        block = ctx.enter_context(nc.Block())

        @block.sync
        def _(sp):
            def load_codes(n):
                if n >= 2:
                    wait(sp, cstep, 0, 8 * (n - 1))
                kind, i = n // 4, n % 4
                if kind < 2:
                    src = (gate_p, up_p)[kind].rearrange("(b p a) j -> p b (a j)", p=P, a=2)[:, 2 * i:2 * i + 2, :]
                    dst = raw[:, n % 2, :].rearrange("p (b j) -> p b j", b=2)
                else:
                    src = down_p.rearrange("(t p) j -> p t j", p=P)[:, i // 2, (i % 2) * 512:(i % 2) * 512 + 512]
                    dst = raw[:, n % 2, :]
                sp.dma_start(dst, src).then_inc(codes_in[n % 2].sem, 16)

            def load_scales(sc, src, landed):
                sp.dma_start(sc[:, :].rearrange("p (b c) -> p b c", b=NF // 2),
                             src.rearrange("(b p a) c -> p b (a c)", p=P, a=2)).then_inc(landed.sem, 16)

            load_codes(0)
            load_scales(g_sc, gate_s, gsc_in)
            sp.dma_start(rows[0:24, :], conv_w.rearrange("i (c p) -> (i c) p", p=P)).then_inc(rows_in.sem, 16)
            sp.dma_start(rows[24:30, :], conv_b.rearrange("(c p) -> c p", p=P)).then_inc(rows_in.sem, 16)
            sp.dma_start(rows[30:34, :], norm_scale.rearrange("(c p) -> c p", p=P)).then_inc(rows_in.sem, 16)
            sp.dma_start(u_sb[:, :, :], u_v[0]).then_inc(u_in.sem, 16)
            sp.dma_start(win_raw, W_in.rearrange("(k p) n -> p k n", p=P)).then_inc(win_in.sem, 16)
            for dst, src in ((dtb, dt_bias), (a_neg, A_log), (d_bc, D)):
                sp.dma_start(dst[:, :], src.partition_broadcast(P)).then_inc(small_in.sem, 16)
            load_codes(1)
            load_scales(u_sc, up_s, sc_in)
            sp.dma_start(d_sc[:, :, :], down_s.rearrange("(t p) b -> p t b", p=P)).then_inc(sc_in.sem, 16)
            sp.dma_start(wout_raw, W_out.rearrange("(j p) d -> p j d", p=P)).then_inc(wout_in.sem, 16)
            for n in range(2, UNITS):
                load_codes(n)

            def wait_for(*rises):
                values = [s.at(g, k) for s, g, k in rises]
                values = [v if isinstance(v, int) else sp.to_reg(v) for v in values]
                sp.wait_ge(win_in.sem, 16)
                for (s, _, _), v in zip(rises, values):
                    sp.wait_ge(s.sem, v)

            def load_u(g):
                wait_for((r_ok, g - 1, 4))
                sp.dma_start(u_sb[:, :, :], u_v[g]).then_inc(u_in.sem, 16)

            def store(f):
                wait_for((o_ok, f, 4))
                sp.dma_start(out_v[f], h_res[:, :, :]).then_inc(stored.sem, 16)

            def keep_h(f):
                wait_for((h_ok, f, 4), *([(stored, f, 0)] if not isinstance(f, int) or f > 0 else []))
                sp.dma_start(h_res[:, :, :], h_sb[:, :, :]).then_inc(hres_ok.sem, 16)

            load_u(1)
            keep_h(0)
            with sp.Fori(1, GROUPS - 1) as g:
                load_u(g + 1)
                store(g - 1)
                keep_h(g)
            store(GROUPS - 2)
            keep_h(GROUPS - 1)
            store(GROUPS - 1)
            wait(sp, stored, GROUPS - 1, 1)

        @block.tensor
        def _(pe):
            def mm3(dst, left, right, first, last):
                (lh, ll), (rh, rl) = left, right
                nc.tensor.matmul(dst, lh, rh, start=first, stop=False, skip_group_check=True)
                nc.tensor.matmul(dst, lh, rl, start=False, stop=False, skip_group_check=True)
                return nc.tensor.matmul(dst, ll, rh, start=False, stop=last, skip_group_check=True)

            def mixer(name, g):
                kind, i = split_name(name)
                if kind == "uT":
                    wait(pe, u_in, g, 1)
                    for k in range(KT):
                        use = f"uT{k}"
                        wait_bank(pe, use, g)
                        for t in range(NT):
                            mm = nc.tensor.transpose(bank(use)[:, t * P:(t + 1) * P],
                                                     u_sb[:, t, k * P:(k + 1) * P], ident[:, :])
                        mm.then_inc(ready(use)[0].sem, 1)
                elif kind == "dt":
                    wait_bank(pe, "dt", g)
                    wait(pe, uT_l, g, 2)
                    for t in range(NT):
                        for k in range(KT):
                            mm = mm3(bank("dt")[:, t * H:(t + 1) * H],
                                     [x[:, k, t * P:(t + 1) * P] for x in (uT_hi, uT_lo)],
                                     [w[:, k, DT0:NIN] for w in (win_hi, win_lo)], k == 0, k == KT - 1)
                    mm.then_inc(ready("dt")[0].sem, 1)
                elif kind == "x":
                    use, c0 = f"x{i}", X0 + i * P
                    wait_bank(pe, use, g)
                    for k in range(KT):
                        mm = mm3(bank(use)[:, :], [w[:, k, c0:c0 + P] for w in (win_hi, win_lo)],
                                 [x[:, k, :] for x in (uT_hi, uT_lo)], k == 0, k == KT - 1)
                    mm.then_inc(ready(use)[0].sem, 1)
                elif kind == "z":
                    use = f"z{i}"
                    wait_bank(pe, use, g)
                    for k in range(KT):
                        mm = mm3(bank(use)[:, :], [x[:, k, i * P:(i + 1) * P] for x in (uT_hi, uT_lo)],
                                 [w[:, k, 0:DI] for w in (win_hi, win_lo)], k == 0, k == KT - 1)
                    mm.then_inc(ready(use)[0].sem, 1)
                elif kind == "CB":
                    use, s = f"CB{i}", i * SEQ
                    wait_bank(pe, use, g)
                    wait(pe, xbc_ok, g, 6)
                    wait(pe, dA_ok, g, 1)
                    b = bank(use)
                    nc.tensor.matmul(b[:, 0:2 * P], xbc[:, 4, s:s + P], xbc[:, 5, s:s + 2 * P],
                                     start=True, stop=True)
                    nc.tensor.matmul(b[:, 2 * P:3 * P], xbc[:, 4, s + P:s + 2 * P], xbc[:, 5, s + P:s + 2 * P],
                                     start=True, stop=True)
                    nc.tensor.matmul(b[:, 3 * P:3 * P + H], tri_r[:, :], dA_hi[:, 2 * i + 1, :],
                                     start=True, stop=False)
                    nc.tensor.matmul(b[:, 3 * P:3 * P + H], tri_r[:, :], dA_lo[:, 2 * i + 1, :],
                                     start=False, stop=True).then_inc(ready(use)[0].sem, 1)
                elif kind == "XT":
                    use = f"XT{i}"
                    wait_bank(pe, use, g)
                    for j in range(JT):
                        mm = nc.tensor.transpose(bank(use)[:, j * P:(j + 1) * P],
                                                 xbc[:, j, i * P:(i + 1) * P], ident[:, :])
                    mm.then_inc(ready(use)[0].sem, 1)
                elif kind == "D":
                    wait(pe, R_ok, g, i + 1)
                    for n, use in enumerate((f"D{i}a", f"D{i}b")):
                        wait_bank(pe, use, g)
                        hs = slice(4 * n, 4 * n + 4)
                        nc.tensor.matmul(bank(use)[:, :], after_r[:, :], R_hi[:, hs, :], start=True, stop=False)
                        nc.tensor.matmul(bank(use)[:, :], after_r[:, :], R_lo[:, hs, :], start=False,
                                         stop=True).then_inc(ready(use)[0].sem, 1)
                elif kind == "Y":
                    use = f"Y{i}"
                    wait_bank(pe, use, g)
                    wait(pe, x_ok, g, i + 1)
                    wait(pe, W_ok, g, i + 1)
                    for h in range(H):
                        mm = nc.tensor.matmul(bank(use)[:, h * HP:(h + 1) * HP], dec[:, h, :],
                                              xdt[:, h * HP:(h + 1) * HP], start=True, stop=True)
                    mm.then_inc(ready(use)[0].sem, 1)
                    if i % 2:
                        use = f"Yoff{i // 2}"
                        wait_bank(pe, use, g)
                        wait(pe, xt_ok, g, i // 2 + 1)
                        nc.tensor.matmul(bank(use)[:, :], cb[:, 1, :], xtail[:, :], start=True,
                                         stop=True).then_inc(ready(use)[0].sem, 1)
                elif kind == "gT":
                    use = f"gT{i}"
                    wait_bank(pe, use, g)
                    wait(pe, y_step, g, (3, 8, 11, 16)[i])
                    for j in range(JT):
                        mm = nc.tensor.transpose(bank(use)[:, j * P:(j + 1) * P],
                                                 zs[:, i, j * P:(j + 1) * P], ident[:, :])
                    mm.then_inc(ready(use)[0].sem, 1)
                elif kind == "op":
                    use = f"op{i}"
                    wait_bank(pe, use, g)
                    wait(pe, gT_l, g, i + 1)
                    for j in range(JT):
                        mm = mm3(bank(use)[:, 0:DM], [x[:, j * P:(j + 1) * P] for x in (gT_hi, gT_lo)],
                                 [w[:, j, :] for w in (wout_hi, wout_lo)], j == 0, j == JT - 1)
                    mm.then_inc(ready(use)[0].sem, 1)

            def down(n, f):
                wait(pe, in_l, f, n + 1)
                for t in range(NT):
                    mm = mm3(OB[t // 2][:, (t % 2) * DM:(t % 2 + 1) * DM],
                             [x[:, n % 2, t * P:(t + 1) * P] for x in (in_hi, in_lo)],
                             [w[:, n, :] for w in (wd_hi, wd_lo)], n == 0 and t % 2 == 0, n == NF - 1)
                mm.then_inc(down_ok.sem, 1)

            def ffn(kind, n, f):
                if kind == "F1":
                    wait(pe, h_ok, f, 4)
                    if isinstance(f, int) and f == 0:
                        pe.wait_ge(wt_lo.sem, 2 * UNITS)
                    else:
                        wait(pe, gelu_ok, f - 1, NF)
                        wait(pe, inter_ok, f - 1, NF)
                    for k, (b, done) in enumerate(((GB, G_ready), (UB, U_ready))):
                        for t in range(NT):
                            mm = nc.tensor.transpose(b[:, t * P:(t + 1) * P], h_sb[:, t, k::2], ident[:, :])
                        mm.then_inc(done.sem, 1)
                elif kind == "unit":
                    if n == 0:
                        wait(pe, hT_l, f, 2)
                    for wh, wl, b, done, read in ((wg_hi, wg_lo, GB, G_ready, gelu_ok),
                                                  (wu_hi, wu_lo, UB, U_ready, inter_ok)):
                        if n:
                            wait(pe, read, f, n)
                        for k in range(KT):
                            mm = mm3(b[:, :], [w[:, k, n * P:(n + 1) * P] for w in (wh, wl)],
                                     [x[:, k, :] for x in (hT_hi, hT_lo)], k == 0, k == KT - 1)
                        mm.then_inc(done.sem, 1)
                    if n >= 2:
                        down(n - 2, f)
                elif kind == "down":
                    down(n, f)

            def first_mixer(name, g):
                if name == "dt":
                    pe.wait_ge(win_ok.sem, 2)
                if name == "op0":
                    pe.wait_ge(wout_ok.sem, 1)
                mixer(name, g)

            def prep(step):
                n = step - 1
                if n < 0:
                    return
                wait(pe, deq, 0, 2 * n + 2)
                for a, (b, done) in enumerate(((GB, G_ready), (UB, U_ready))):
                    if n:
                        pe.wait_ge(wt_lo.sem, 2 * n - 1 + a)
                    for q in range(4):
                        mm = nc.tensor.matmul(b[:, q * P:(q + 1) * P], wdq[:, a, q * P:(q + 1) * P], ident[:, :],
                                              start=q == 0, stop=False, skip_group_check=True)
                    mm.then_inc(done.sem, 1)
                for a, (b, done) in enumerate(((GB, G_ready), (UB, U_ready))):
                    pe.wait_ge(wt_hi.sem, 2 * n + a + 1)
                    nc.tensor.matmul(b[:, :], minus_ident_r[:, :], prep_dst(n, a)[0], start=False, stop=True,
                                     skip_group_check=True).then_inc(done.sem, 1)

            pe.wait_ge(consts.sem, 5)
            pe.wait_ge(rows_in.sem, 16 * 3)
            nc.tensor.transpose(MB[0][:, 0:34], rows, ident[0:34, 0:34]).then_inc(bank_ready[0].sem, 1)
            pe.wait_ge(crt.sem, 5)
            mixer("uT", 0)
            run(0, False, first_mixer, ffn, prep)
            with pe.Fori(1, GROUPS - 1) as g:
                run(g, False, mixer, ffn)
            run(GROUPS - 1, True, mixer, ffn)
            run_end(ffn)

        @block.scalar
        def _(act):
            def tanh(n, g):
                c = CONV_ORDER[n]
                wait(act, conv, g, 3 * n + 3)
                wait(act, ssq_ok, g - 1, NT)
                if n >= 2:
                    wait(act, xbc_ok, g, n - 1)
                nc.scalar.activation(y[:, n % 2, :], xbc[:, c, :], ACT.Tanh).then_inc(x_tanh.sem, 1)

            def mixer(name, g):
                kind, i = split_name(name)
                if kind == "uT":
                    wait_ready(act, "D3b", g - 1)
                    for k in range(KT):
                        wait_ready(act, f"uT{k}", g)
                        nc.scalar.activation(uT_hi[:, k, :], bank(f"uT{k}")[:, :], ACT.Copy).then_inc(uT_h.sem, 1)
                elif kind == "dt":
                    wait(act, dt_step, g, 2)
                    nc.scalar.activation(dte[:, :], dta[:, :], ACT.Exp).then_inc(dt_exp.sem, 1)
                elif kind == "x":
                    n = CONV_ORDER.index(i)
                    wait_ready(act, f"x{i}", g)
                    wait_ready(act, "XT3", g - 1)
                    nc.scalar.activation(xbc[:, i, :], bank(f"x{i}")[:, :], ACT.Identity,
                                         bias=chan[:, 24 + i:25 + i],
                                         scale=chan[:, 18 + i:19 + i]).then_inc(conv0.sem, 1)
                    if n:
                        tanh(n - 1, g)
                elif kind == "z":
                    if i == 0:
                        tanh(CT - 1, g)
                    wait_ready(act, f"z{i}", g)
                    wait_ready(act, f"gT{i}", g - 1)
                    wait(act, ssq_ok, g - 1, i + 1)
                    nc.scalar.activation(zs[:, i, :], bank(f"z{i}")[:, :], ACT.Tanh, scale=0.5)\
                        .then_inc(z_tanh.sem, 1)
                elif kind == "CB":
                    wait_ready(act, f"CB{i}", g)
                    if i:
                        wait_ready(act, "Yoff0", g)
                    else:
                        wait_ready(act, "Yoff1", g - 1)
                    nc.scalar.activation(cb[:, 1, :], bank(f"CB{i}")[:, P:2 * P], ACT.Copy)
                    nc.scalar.activation(e2[:, i, :], bank(f"CB{i}")[:, 3 * P:3 * P + H],
                                         ACT.Exp).then_inc(cb_act.sem, 1)
                elif kind == "D":
                    if i:
                        wait_ready(act, f"Y{i - 1}", g)
                    else:
                        wait_ready(act, "Y3", g - 1)
                    for n, use in enumerate((f"D{i}a", f"D{i}b")):
                        wait_ready(act, use, g)
                        nc.scalar.activation(dec[:, 4 * n:4 * n + 4, :],
                                             bank(use)[:, :].rearrange("p (h l) -> p h l", h=4),
                                             ACT.Exp).then_inc(dec_ok.sem, 1)
                elif kind == "gT":
                    wait(act, y_step, g, (3, 8, 11, 16)[i])
                    nc.scalar.activation(y[:, i % 2, :], zs[:, i, :], ACT.Square,
                                         accum_out=ssq[:, i:i + 1]).then_inc(ssq_ok.sem, 1)
                    wait_ready(act, f"gT{i}", g)
                    if i:
                        wait_ready(act, f"op{i - 1}", g)
                    else:
                        wait_ready(act, "op3", g - 1)
                    nc.scalar.activation(gT_hi[:, :], bank(f"gT{i}")[:, :], ACT.Copy).then_inc(gT_h.sem, 1)

            def inter_hi(n, f):
                wait(act, inter_ok, f, n + 1)
                if n >= 2:
                    wait(act, down_ok, f, n - 1)
                nc.scalar.activation(in_hi[:, n % 2, :], act_sb[:, n % 2, :], ACT.Copy).then_inc(in_h.sem, 1)

            def ffn(kind, n, f):
                if kind == "F1":
                    for k, (b, done) in enumerate(((GB, G_ready), (UB, U_ready))):
                        wait(act, done, f, 1)
                        nc.scalar.activation(hT_hi[:, k, :], b[:, :], ACT.Copy).then_inc(hT_h.sem, 1)
                elif kind == "unit":
                    if n:
                        inter_hi(n - 1, f)
                    wait(act, G_ready, f, n + 2)
                    if n >= 2:
                        wait(act, in_l, f, n - 1)
                    nc.scalar.activation(act_sb[:, n % 2, :], GB[:, :], ACT.Gelu_apprx_tanh).then_inc(gelu_ok.sem, 1)
                elif kind == "down" and n == NF - 2:
                    inter_hi(NF - 1, f)

            def prep(step):
                n = step - 1
                if n < 0:
                    return
                for part, signal in ((0, wt_hi), (1, wt_lo)):
                    for a, (b, done) in enumerate(((GB, G_ready), (UB, U_ready))):
                        act.wait_ge(done.sem, 2 * n + 1 + part)
                        nc.scalar.activation(prep_dst(n, a)[part], b[:, :].rearrange("p (q m) -> p q m", q=4),
                                             ACT.Copy).then_inc(signal.sem, 1)

            def first_mixer(name, g):
                if name == "x4":
                    act.wait_ge(crt.sem, 5)
                    act.wait_ge(win_ok.sem, 2)
                if name == "x2":
                    act.wait_ge(wsc.sem, 4)
                    nc.scalar.activation(wout_hi[:, :, :], wout_raw, ACT.Copy).then_inc(wout_top.sem, 1)
                if name == "z0":
                    act.wait_ge(wout_ok.sem, 1)
                mixer(name, g)

            act.wait_ge(win_in.sem, 16)
            for k in range(KT):
                nc.scalar.activation(win_hi[:, k, :], win_raw[:, k, :], ACT.Copy).then_inc(win_top.sem, 1)
            mixer("uT", 0)
            act.wait_ge(small_in.sem, 16 * 3)
            nc.scalar.activation(a_neg[:, :], a_neg[:, :], ACT.Exp).then_inc(a_exp.sem, 1)
            run(0, False, first_mixer, ffn, prep)
            with act.Fori(1, GROUPS - 1) as g:
                run(g, False, mixer, ffn)
            run(GROUPS - 1, True, mixer, ffn)
            run_end(ffn)

        @block.vector
        def _(dve):
            tt, ts, stt = nc.vector.tensor_tensor, nc.vector.tensor_scalar, nc.vector.scalar_tensor_tensor

            def head(ap):
                return ap.rearrange("p (h c) -> p h c", h=H)

            def silu(n, g):
                c = CONV_ORDER[n]
                wait(dve, x_tanh, g, n + 1)
                stt(xbc[:, c, :], y[:, n % 2, :], 1.0, xbc[:, c, :], ALU.add, ALU.mult).then_inc(xbc_ok.sem, 1)

            def dt_chain(k, g):
                if k:
                    wait(dve, dt_step, g, k)
                flat = dt_sb[:, :, :].rearrange("p t h -> p (t h)")
                if k == 0:
                    wait_ready(dve, "dt", g)
                    ins = tt(dtx[:, :].rearrange("p (t h) -> p t h", t=NT),
                             bank("dt")[:, 0:NT * H].rearrange("p (t h) -> p t h", t=NT),
                             dtb[:, :].unsqueeze(1).to_broadcast([P, NT, H]), ALU.add)
                elif k == 1:
                    ins = stt(dta[:, :], dtx[:, :], -1.0, dtx[:, :], ALU.mult, ALU.min)
                elif k == 2:
                    ins = ts(dtx[:, :], dtx[:, :], 0.0, None, ALU.max)
                elif k == 3:
                    wait(dve, dt_exp, g, 1)
                    ins = ts(dtp[:, :], dte[:, :], 2.0, None, ALU.add)
                elif k == 4:
                    ins = nc.vector.reciprocal(dtp[:, :], dtp[:, :])
                elif k == 5:
                    ins = tt(dts[:, :], dte[:, :], dtp[:, :], ALU.mult)
                elif k == 6:
                    ins = tt(dtq[:, :], dts[:, :], dts[:, :], ALU.mult)
                elif k == 7:
                    ins = ts(dtp[:, :], dtq[:, :], 1.0 / 17, None, ALU.mult)
                elif k <= 14:
                    ins = stt(dtp[:, :], dtp[:, :], 1.0 / (31 - 2 * k), dtq[:, :], ALU.add, ALU.mult)
                elif k == 15:
                    ins = stt(dtp[:, :], dtp[:, :], 1.0, dts[:, :], ALU.add, ALU.mult)
                elif k == 16:
                    ins = stt(flat, dtp[:, :], 2.0, dtx[:, :], ALU.mult, ALU.add)
                elif k == 17:
                    ins = tt(dA[:, :, :], dt_sb[:, :, :], a_neg[:, :].unsqueeze(1).to_broadcast([P, NT, H]),
                             ALU.mult)
                elif k == 18:
                    ins = nc.vector.tensor_copy(dA_hi[:, :, :], dA[:, :, :])
                else:
                    ins = tt(dA_lo[:, :, :], dA[:, :, :], f32(dA_hi[:, :, :]), ALU.subtract)
                ins.then_inc(dA_ok.sem if k == 19 else dt_step.sem, 1)

            def mixer(name, g):
                kind, i = split_name(name)
                if kind == "uT":
                    for k in range(KT):
                        wait(dve, uT_h, g, k + 1)
                        tt(uT_lo[:, k, :], bank(f"uT{k}")[:, :], f32(uT_hi[:, k, :]), ALU.subtract)\
                            .then_inc(uT_l.sem, 1)
                elif kind == "dt":
                    dt_chain(0, g)
                    dt_chain(1, g)
                elif kind == "x":
                    n = CONV_ORDER.index(i)
                    acc = xbc[:, i, :].rearrange("p (q s) -> p q s", q=2)
                    src = bank(f"x{i}")[:, :].rearrange("p (q s) -> p q s", q=2)
                    wait(dve, conv0, g, n + 1)
                    for d in (1, 2, 3):
                        c = (3 - d) * CT + i
                        ins = stt(acc[:, :, d:], src[:, :, 0:SEQ - d], chan[:, c:c + 1], acc[:, :, d:],
                                  ALU.mult, ALU.add)
                        ins.then_inc(conv.sem, 1)
                        dt_chain(3 * n + d + 1, g)
                        wait(dve, conv, g, 3 * n + d)
                    if n:
                        silu(n - 1, g)
                elif kind == "z":
                    if i == 0:
                        silu(CT - 1, g)
                    wait(dve, z_tanh, g, i + 1)
                    stt(zs[:, i, :], zs[:, i, :], 1.0, bank(f"z{i}")[:, :], ALU.add, ALU.mult)\
                        .then_inc(zs_ok.sem, 1)
                elif kind == "CB":
                    wait(dve, cb_act, g, i + 1)
                    tt(cb[:, 0, :], bank(f"CB{i}")[:, 0:P], tri[:, :], ALU.mult)
                    tt(cb[:, 2, :], bank(f"CB{i}")[:, 2 * P:3 * P], tri[:, :], ALU.mult).then_inc(cb_ok.sem, 1)
                elif kind == "XT":
                    use = f"XT{i}"
                    wait_ready(dve, use, g)
                    wait(dve, ssq_ok, g, i - 1)
                    tt(head(y[:, i % 2, :]), head(bank(use)[:, :]),
                       d_bc[:, :].unsqueeze(2).to_broadcast([P, H, HP]), ALU.mult).then_inc(y_step.sem, 1)
                    tt(head(xdt[:, :]), head(bank(use)[:, :]),
                       dt_sb[:, i, :].unsqueeze(2).to_broadcast([P, H, HP]), ALU.mult).then_inc(x_ok.sem, 1)
                elif kind == "D":
                    wait(dve, dec_ok, g, 2 * i + 2)
                    if i % 2 == 0:
                        wait(dve, x_ok, g, i + 1)
                        tt(head(xtail[:, :]), head(xdt[:, :]), dec[:, :, P - 1:P].to_broadcast([P, H, HP]),
                           ALU.mult).then_inc(xt_ok.sem, 1)
                        wait(dve, xt_ok, g, i // 2 + 1)
                    wait(dve, cb_ok, g, i // 2 + 1)
                    tt(dec[:, :, :], dec[:, :, :], cb[:, 2 * (i % 2):2 * (i % 2) + 1, :].to_broadcast([P, H, P]),
                       ALU.mult).then_inc(W_ok.sem, 1)
                elif kind == "Y":
                    s0 = (0, 3, 8, 11)[i]
                    yc = y[:, i % 2, :]
                    wait_ready(dve, f"Y{i}", g)
                    wait(dve, y_step, g, s0 + 1)
                    tt(yc, bank(f"Y{i}")[:, :], yc, ALU.add).then_inc(y_step.sem, 1)
                    wait(dve, y_step, g, s0 + 2)
                    s0 += 2
                    if i % 2:
                        use = f"Yoff{i // 2}"
                        wait_ready(dve, use, g)
                        tt(head(xdt[:, :]), head(bank(use)[:, :]),
                           e2[:, i // 2, :].unsqueeze(2).to_broadcast([P, H, HP]), ALU.mult)\
                            .then_inc(y_step.sem, 1)
                        wait(dve, y_step, g, s0 + 1)
                        tt(yc, yc, xdt[:, :], ALU.add).then_inc(y_step.sem, 1)
                        wait(dve, y_step, g, s0 + 2)
                    wait(dve, zs_ok, g, i + 1)
                    tt(zs[:, i, :], zs[:, i, :], yc, ALU.mult).then_inc(y_step.sem, 1)
                elif kind == "gT":
                    wait(dve, gT_h, g, i + 1)
                    tt(gT_lo[:, :], bank(f"gT{i}")[:, :], f32(gT_hi[:, :]), ALU.subtract).then_inc(gT_l.sem, 1)
                elif kind == "op":
                    if i == 0:
                        wait(dve, hres_ok, g, 0)
                    wait_ready(dve, f"op{i}", g)
                    wait(dve, rms_step, g, 3 * i + 3)
                    stt(h_sb[:, i, :], bank(f"op{i}")[:, 0:DM], rms[:, i:i + 1], u_sb[:, i, :],
                        ALU.mult, ALU.add).then_inc(r_ok.sem, 1)
                elif kind == "ln":
                    norm(h_sb, bn6, mv, lnr, (r_ok, ln_bn, ln_mv, ln_pow, h_ok), g)

            def norm(x, six, two, rs, signals, g):
                summed, stats, moments, power, done = signals
                for t in range(NT):
                    wait(dve, summed, g, t + 1)
                    nc.vector.bn_stats(six[:, t, :], x[:, t, :]).then_inc(stats.sem, 1)
                for t in range(NT):
                    dve.wait_ge(consts.sem, 5)
                    wait(dve, stats, g, t + 1)
                    nc.vector.bn_aggr(two[:, t, :], six[:, t, :]).then_inc(moments.sem, 1)
                wait(dve, moments, g, 4)
                wait(dve, power, g, 2)
                for t in range(NT):
                    ts(x[:, t, :], x[:, t, :], two[:, t, 0:1], rs[:, t:t + 1], ALU.subtract, ALU.mult)\
                        .then_inc(done.sem, 1)

            def inter_lo(n, f):
                wait(dve, in_h, f, n + 1)
                tt(in_lo[:, n % 2, :], act_sb[:, n % 2, :], f32(in_hi[:, n % 2, :]), ALU.subtract)\
                    .then_inc(in_l.sem, 1)

            def ffn(kind, n, f):
                if kind == "F1":
                    for k, b in enumerate((GB, UB)):
                        wait(dve, hT_h, f, k + 1)
                        tt(hT_lo[:, k, :], b[:, :], f32(hT_hi[:, k, :]), ALU.subtract).then_inc(hT_l.sem, 1)
                elif kind == "unit":
                    if n:
                        inter_lo(n - 1, f)
                    wait(dve, gelu_ok, f, n + 1)
                    wait(dve, U_ready, f, n + 2)
                    tt(act_sb[:, n % 2, :], UB[:, :], act_sb[:, n % 2, :], ALU.mult).then_inc(inter_ok.sem, 1)
                elif kind == "down" and n == NF - 2:
                    inter_lo(NF - 1, f)
                elif kind == "final":
                    wait(dve, down_ok, f, NF)
                    wait(dve, hres_ok, f, 1)
                    for t in range(NT):
                        tt(h_res[:, t, :], OB[t // 2][:, (t % 2) * DM:(t % 2 + 1) * DM], h_res[:, t, :],
                           ALU.add).then_inc(o_sum.sem, 1)
                    norm(h_res, fbn6, fmv, flnr, (o_sum, o_bn, o_mv, o_pow, o_ok), f)

            def prep(n):
                if n == UNITS:
                    return
                src = raw16[:, n % 2, :]
                c2 = code.rearrange("p a j -> p (a j)")
                o2 = other.rearrange("p a j -> p (a j)")
                s0 = 8 * n
                dve.wait_ge(codes_in[n % 2].sem, 16 * (n // 2 + 1))
                if n:
                    wait(dve, deq, 0, 2 * n)
                ts(code[:, 0, :], src, 7, 6, ALU.bitwise_and, ALU.logical_shift_left).then_inc(cstep.sem, 1)
                ts(code[:, 1, :], src, 0x70, 2, ALU.bitwise_and, ALU.logical_shift_left).then_inc(cstep.sem, 1)
                wait(dve, cstep, 0, s0 + 2)
                ts(c2, c2, QUARTER_BITS, None, ALU.bitwise_or).then_inc(cstep.sem, 1)
                wait(dve, cstep, 0, s0 + 3)
                ts(o2.bitcast(BF16), c2.bitcast(BF16), 2.0, -0.25, ALU.mult, ALU.add).then_inc(cstep.sem, 1)
                wait(dve, cstep, 0, s0 + 4)
                tt(c2.bitcast(BF16), c2.bitcast(BF16), o2.bitcast(BF16), ALU.min).then_inc(cstep.sem, 1)
                wait(dve, cstep, 0, s0 + 5)
                ts(other[:, 0, :], src, 8, 12, ALU.bitwise_and, ALU.logical_shift_left).then_inc(cstep.sem, 1)
                ts(other[:, 1, :], src, 0x80, 8, ALU.bitwise_and, ALU.logical_shift_left).then_inc(cstep.sem, 1)
                wait(dve, cstep, 0, s0 + 7)
                tt(c2, c2, o2, ALU.bitwise_or).then_inc(cstep.sem, 1)

            def first_mixer(name, g):
                if name == "dt":
                    dve.wait_ge(a_exp.sem, 1)
                    ts(a_neg[:, :], a_neg[:, :], -1.0, None, ALU.mult).then_inc(a_ready.sem, 1)
                    dve.wait_ge(a_ready.sem, 1)
                if name == "x0":
                    dve.wait_ge(wout_in.sem, 16)
                    for j in range(JT):
                        ts(wout_raw[:, j, :], wout_raw[:, j, :], chan[:, 30 + j:31 + j], None, ALU.mult)\
                            .then_inc(wsc.sem, 1)
                if name == "x3":
                    dve.wait_ge(wout_top.sem, 1)
                    tt(wout_lo[:, :, :], wout_raw, f32(wout_hi[:, :, :]), ALU.subtract).then_inc(wout_ok.sem, 1)
                if name == "op0":
                    dve.wait_ge(U_ready.sem, 2 * UNITS - 1)
                mixer(name, g)

            dve.wait_ge(consts.sem, 5)
            nc.vector.tensor_copy(tri_r[:, :], tri[:, :]).then_inc(crt.sem, 1)
            ts(after_r[:, :], tri[:, :], -1.0, 1.0, ALU.mult, ALU.add).then_inc(crt.sem, 1)
            ts(minus_ident_r[:, :], ident[:, :], -1.0, None, ALU.mult).then_inc(crt.sem, 1)
            prep(0)
            dve.wait_ge(bank_ready[0].sem, 1)
            ts(chan[:, 0:30], MB[0][:, 0:30], 0.5, None, ALU.mult).then_inc(crt.sem, 1)
            nc.vector.tensor_copy(chan[:, 30:34], MB[0][:, 30:34]).then_inc(crt.sem, 1)
            dve.wait_ge(crt.sem, 5)
            for k in range(KT):
                dve.wait_ge(win_top.sem, k + 1)
                tt(win_lo[:, k, :], win_raw[:, k, :], f32(win_hi[:, k, :]), ALU.subtract).then_inc(win_ok.sem, 1)
            mixer("uT", 0)
            run(0, False, first_mixer, ffn, prep)
            with dve.Fori(1, GROUPS - 1) as g:
                run(g, False, mixer, ffn)
            run(GROUPS - 1, True, mixer, ffn)
            run_end(ffn)

        @block.gpsimd
        def _(pool):
            tt, ts = nc.gpsimd.tensor_tensor, nc.gpsimd.tensor_scalar

            def rsqrt(dst, tmp, var, least, signal, g, k, n):
                tt(tmp, var, least, ALU.add).then_inc(signal.sem, 1)
                wait(pool, signal, g, k)
                tt(dst, tmp, half[:, 0:n], ALU.pow).then_inc(signal.sem, 1)

            def mixer(name, g):
                kind, i = split_name(name)
                if kind == "R":
                    if i:
                        wait_ready(pool, f"D{i - 1}b", g)
                    else:
                        wait_ready(pool, "z3", g)
                    wait(pool, dA_ok, g, 1)
                    mask = tri[:, :].unsqueeze(1).to_broadcast([P, H, P])
                    for R, step in ((R_hi, dA_hi), (R_lo, dA_lo)):
                        ins = tt(R, mask, f32(step[:, i, :]).unsqueeze(2).to_broadcast([P, H, P]), ALU.mult)
                    ins.then_inc(R_ok.sem, 1)
                elif kind == "gT":
                    wait(pool, ssq_ok, g, i + 1)
                    tt(ms[:, i:i + 1], ssq[:, i:i + 1], inv_di[:, :], ALU.mult).then_inc(rms_step.sem, 1)
                    wait(pool, rms_step, g, 3 * i + 1)
                    rsqrt(rms[:, i:i + 1], rms_v[:, i:i + 1], ms[:, i:i + 1], eps4[:, :], rms_step, g,
                          3 * i + 2, 1)
                elif kind == "ln":
                    wait(pool, ln_mv, g, 4)
                    rsqrt(lnr[:, :], lnv[:, :], mv[:, :, 1], eps[:, :], ln_pow, g, 1, NT)

            def ffn(kind, n, f):
                if kind == "final":
                    wait(pool, o_mv, f, 4)
                    rsqrt(flnr[:, :], flnv[:, :], fmv[:, :, 1], eps[:, :], o_pow, f, 1, NT)

            def prep(n):
                if n == UNITS:
                    return
                sc = (g_sc[:, (n % 4) * 32:(n % 4 + 1) * 32], u_sc[:, (n % 4) * 32:(n % 4 + 1) * 32],
                      d_sc[:, (n % 4) // 2, (n % 2) * 32:(n % 2 + 1) * 32])[n // 4]
                wait(pool, cstep, 0, 8 * n + 8)
                if n:
                    pool.wait_ge(U_ready.sem, 2 * n - 1)
                for a in range(2):
                    tt(wdq[:, a, :].rearrange("p (b k) -> p b k", b=32),
                       code[:, a, :].bitcast(BF16).rearrange("p (b k) -> p b k", b=32),
                       sc.unsqueeze(2).to_broadcast([P, 32, 16]), ALU.mult).then_inc(deq.sem, 1)

            nc.gpsimd.memset(ident[:, :], 0.0).then_inc(consts.sem, 1)
            nc.gpsimd.memset(tri[:, :], 1.0).then_inc(consts.sem, 1)
            nc.gpsimd.memset(half[:, :], -0.5)
            nc.gpsimd.memset(eps[:, :], EPS)
            nc.gpsimd.memset(eps4[:, :], 4 * EPS)
            nc.gpsimd.memset(inv_di[:, :], 1.0 / DI).then_inc(consts.sem, 1)
            pool.wait_ge(consts.sem, 3)
            nc.gpsimd.affine_select(out=ident[:, :], in_=ident[:, :], compare_op=ALU.not_equal, fill=1.0, base=0,
                                    pattern=[[-1, P]], channel_multiplier=1).then_inc(consts.sem, 1)
            nc.gpsimd.affine_select(out=tri[:, :], in_=tri[:, :], compare_op=ALU.is_ge, fill=0.0, base=0,
                                    pattern=[[1, P]], channel_multiplier=-1).then_inc(consts.sem, 1)
            pool.wait_ge(consts.sem, 5)
            pool.wait_ge(gsc_in.sem, 16)
            ts(g_sc[:, :], g_sc[:, :], 4.0, None, ALU.mult).then_inc(quad.sem, 1)
            pool.wait_ge(quad.sem, 1)
            prep(0)
            pool.wait_ge(sc_in.sem, 16 * 2)
            for sc in (u_sc[:, :], d_sc[:, :, :]):
                ts(sc, sc, 4.0, None, ALU.mult).then_inc(quad.sem, 1)
            pool.wait_ge(quad.sem, 3)
            run(0, False, mixer, ffn, prep)
            with pool.Fori(1, GROUPS - 1) as g:
                run(g, False, mixer, ffn)
            run(GROUPS - 1, True, mixer, ffn)
            run_end(ffn)


_INS = ["L0_attn_u", "L0_attn_W_in", "L0_attn_conv_w", "L0_attn_conv_b", "L0_attn_dt_bias", "L0_attn_A_log",
        "L0_attn_D", "L0_attn_norm_scale", "L0_attn_W_out", "L0_ffn_gate_W_packed", "L0_ffn_gate_scales",
        "L0_ffn_up_W_packed", "L0_ffn_up_scales", "L0_ffn_down_W_packed", "L0_ffn_down_scales"]
_OUTS = [((16, 256, 256), "float32")]


def kernel(**inputs):
    import numpy as _np
    import concourse.bacc as _bacc
    from concourse import mybir as _mybir
    from concourse.bass_utils import run_bass_kernel_spmd as _run

    nc = _bacc.Bacc("TRN2", target_bir_lowering=False, num_devices=1)
    arrays, args = {}, []
    for name in _INS:
        a = _np.ascontiguousarray(inputs[name])
        arrays[f"in_{name}_dram"] = a
        args.append(nc.dram_tensor(f"in_{name}_dram", a.shape, _mybir.dt.from_np(a.dtype), kind="ExternalInput").ap())
    for i, (shape, dtype) in enumerate(_OUTS):
        dt = _mybir.dt.from_np(_np.dtype(dtype))
        args.append(nc.dram_tensor(f"out_{i}_dram", shape, dt, kind="ExternalOutput").ap())
    mamba_ffn_kernel(nc, *args)
    r = _run(nc, [arrays], core_ids=[0])
    got = tuple(r.results[0][f"out_{i}_dram"] for i in range(len(_OUTS)))
    return got[0]
```

```python
from contextlib import ExitStack

import concourse.bass as bass
from concourse import mybir

ALU = mybir.AluOpType
ACT = mybir.ActivationFunctionType
F32 = mybir.dt.float32
F32R = mybir.dt.float32r
I32 = mybir.dt.int32
U8 = mybir.dt.uint8
BF16 = mybir.dt.bfloat16

P = 128
EPS = 1e-5
QUARTER_BITS = 124 << 7
SPREAD = 2**6 + 2**18
MAGNITUDES, SIGNS = 0x01C001C0, 0x80008000 - 2**32

USES = (["uT0", "uT1", "dt", "x4", "x5", "x0", "z0", "x1", "z1", "x2", "z2", "x3", "z3", "CB0", "XT0",
         "D0a", "D0b", "Y0", "XT1", "D1a", "D1b", "Y1", "Yoff0", "CB1", "gT0", "XT2", "D2a", "D2b",
         "op0", "gT1", "Y2", "XT3", "D3a", "D3b", "op1", "gT2", "Y3", "Yoff1", "op2", "gT3", "op3"])
CONV_ORDER = (4, 5, 0, 1, 2, 3)
SLOTS = [[], ["x5", "x0", "z0"], ["x1", "z1"], ["x2", "z2"], ["x3", "z3"], ["CB0", "R0", "XT0"],
         ["D0"], ["R1", "Y0", "XT1"], ["D1"], ["R2", "Y1", "CB1", "gT0", "XT2"], ["D2"],
         ["R3", "op0", "gT1", "Y2", "XT3"], ["D3"], ["op1", "gT2", "Y3"], ["op2", "gT3"], ["op3", "ln1"], ["ln2"]]
BEFORE_H = [n for n, slot in enumerate(SLOTS) if "op0" in slot][0]


def stages(kind, units, slots):
    order, at = [], 0
    for n, slot in enumerate(SLOTS):
        order += [("mixer", name) for name in slot]
        upto = min((n + 1) * len(units) // slots, len(units))
        order += [(kind, r) for r in units[at:upto]]
        at = upto
    return order


def split_name(name):
    kind = name.rstrip("0123456789")
    return kind, int(name[len(kind):] or 0)


class Signal:

    def __init__(self, sem, per, base=0, step=1):
        self.sem, self.per, self.base, self.step = sem, per, base, step

    def at(self, group, k):
        return group * (self.per * self.step) + (self.base + k) * self.step


def wait(eng, signal, group, k):
    value = signal.at(group, k)
    if not isinstance(value, int) or value > 0:
        eng.wait_ge(signal.sem, value)


def mamba_ffn_kernel(nc, u, W_in, conv_w, conv_b, dt_bias, A_log, D, norm_scale, W_out,
                     gate_p, gate_s, up_p, up_s, down_p, down_s, out):
    BATCH, SEQ, DM = u.shape
    DI = norm_scale.shape[0]
    H = D.shape[0]
    HP = DI // H
    NIN = W_in.shape[1]
    FF = gate_p.shape[0]
    TOK = 512
    NT = TOK // P
    GROUPS = BATCH * SEQ // TOK
    KT = DM // P
    JT = DI // P
    CT = (NIN - H - DI) // P
    NF = FF // P
    UNITS = 12
    STEPS = 6
    X0, DT0 = DI, NIN - H
    assert (SEQ, TOK // SEQ, KT, JT, CT, NF) == (256, 2, 2, 4, 6, 16)

    u_v = u.rearrange("b s d -> (b s) d").rearrange("(g t p) d -> g p t d", t=NT, p=P)
    out_v = out.rearrange("b s d -> (b s) d").rearrange("(g t p) d -> g p t d", t=NT, p=P)

    with ExitStack() as ctx:
        def sb(name, shape, dt=F32):
            return ctx.enter_context(nc.sbuf_tensor(name, shape, dt))

        def sig(name, per, base=0, step=1):
            return Signal(ctx.enter_context(nc.semaphore(name)), per, base, step)

        win_hi, win_lo = sb("win_hi", [P, KT, NIN], F32R), sb("win_lo", [P, KT, NIN], F32R)
        wdt = sb("wdt", [P, KT, 2, H], F32R)
        wout_hi, wout_lo = sb("wout_hi", [P, JT, DM], F32R), sb("wout_lo", [P, JT, DM], F32R)
        wg_hi, wg_lo = sb("wg_hi", [P, KT, FF], F32R), sb("wg_lo", [P, KT, FF], F32R)
        wu_hi, wu_lo = sb("wu_hi", [P, KT, FF], F32R), sb("wu_lo", [P, KT, FF], F32R)
        wd_hi, wd_lo = sb("wd_hi", [P, NF, DM], F32R), sb("wd_lo", [P, NF, DM], F32R)
        ident = sb("ident", [P, P])
        tri = sb("tri", [P, P])
        tri_r = sb("tri_r", [P, P], F32R)
        minus_ident_r = sb("minus_ident_r", [P, P], F32R)
        after_r = sb("after_r", [P, P], F32R)
        chan = sb("chan", [P, 34])
        dtb, a_neg, d_bc = sb("dtb", [P, H]), sb("a_neg", [P, H]), sb("d_bc", [P, H])
        half, eps, inv_di = sb("minus_half", [P, NT]), sb("eps", [P, NT]), sb("inv_di", [P, 1])
        eps4 = sb("eps4", [P, 1])
        g_sc, u_sc = sb("g_sc", [P, NF * 8]), sb("u_sc", [P, NF * 8])
        d_sc = sb("d_sc", [P, 2, 64])
        u_sb = sb("u_sb", [P, NT, DM])
        uT_hi, uT_lo = sb("uT_hi", [P, KT, TOK], F32R), sb("uT_lo", [P, KT, TOK], F32R)
        R_hi = uT_hi[:, :, :].rearrange("p k (h l) -> p (k h) l", l=P)
        R_lo = uT_lo[:, :, :].rearrange("p k (h l) -> p (k h) l", l=P)
        xbc = sb("xbc", [P, CT, TOK])
        zs = sb("zs", [P, NT, DI])
        dtx, dte = sb("dtx", [P, NT * H]), sb("dte", [P, NT * H])
        dts, dtq, dtp = sb("dts", [P, NT * H]), sb("dtq", [P, NT * H]), sb("dtp", [P, NT * H])
        dt_sb, dA = sb("dt_sb", [P, NT, H]), sb("dA", [P, NT, H])
        dA_hi, dA_lo = sb("dA_hi", [P, NT, H], F32R), sb("dA_lo", [P, NT, H], F32R)
        dec = sb("dec", [P, H, P])
        cb = sb("cb", [P, 3, P])
        e2 = sb("e2", [P, 2, H])
        xdt, xtail = sb("xdt", [P, DI]), sb("xtail", [P, DI])
        y = sb("y", [P, 2, DI])
        ssq, ms, rms_v, rms = (sb(name, [P, NT]) for name in ("ssq", "mean_square", "rms_v", "rms"))
        gT_hi, gT_lo = sb("gT_hi", [P, DI], F32R), sb("gT_lo", [P, DI], F32R)
        bn6, mv = sb("bn6", [P, NT, 6]), sb("mv", [P, NT, 2])
        lnv, lnr = sb("lnv", [P, NT]), sb("lnr", [P, NT])
        h_sb = sb("h_sb", [P, NT, DM])
        h_res = sb("h_res", [P, NT, DM])
        hT_hi, hT_lo = sb("hT_hi", [P, KT, TOK], F32R), sb("hT_lo", [P, KT, TOK], F32R)
        act_sb = sb("act_sb", [P, 2, TOK])
        in_hi, in_lo = sb("in_hi", [P, 2, TOK], F32R), sb("in_lo", [P, 2, TOK], F32R)
        fbn6, fmv = sb("fbn6", [P, NT, 6]), sb("fmv", [P, NT, 2])
        flnv, flnr = sb("flnv", [P, NT]), sb("flnr", [P, NT])
        win_raw = xbc[:, :, :].rearrange("p c t -> p (c t)")[:, 0:KT * NIN].rearrange("p (k n) -> p k n", k=KT)
        wout_raw = zs[:, 2:4, :].rearrange("p a (b d) -> p (a b) d", d=DM)
        rows = y[0:34, 0, 0:P]
        raw = h_res[:, :, :].rearrange("p (b a) d -> p b (a d)", b=2).bitcast(I32)
        raw8 = h_res[:, :, :].rearrange("p (b a) d -> p b (a d)", b=2).bitcast(U8)\
            .rearrange("p b (d w) -> p b d w", w=4)[:, :, :, 0]
        code, other = act_sb[:, 0, :].bitcast(I32), act_sb[:, 1, :].bitcast(I32)
        wdq = h_sb[:, :, :].rearrange("p (a b) d -> p a (b d)", a=2)

        MB = [ctx.enter_context(nc.psum_tensor(f"mixer{b}", [P, 512], F32)) for b in range(4)]
        GB = ctx.enter_context(nc.psum_tensor("gate_bank", [P, 512], F32))
        UB = ctx.enter_context(nc.psum_tensor("up_bank", [P, 512], F32))
        OB = [ctx.enter_context(nc.psum_tensor(f"down{b}", [P, 512], F32)) for b in range(2)]

        per_bank = [len(USES[b::4]) for b in range(4)]
        bank_ready = [sig(f"mixer{b}_ready", per_bank[b], base=1 if b == 0 else 0) for b in range(4)]
        rows_in = sig("rows_in", 0, step=16)
        small_in = sig("small_in", 0, step=16)
        gsc_in, sc_in = sig("gate_scales_in", 0, step=16), sig("scales_in", 0, step=16)
        win_in = [sig(f"win_in{k}", 0, step=16) for k in range(KT)]
        wout_in = sig("wout_in", 0, step=16)
        codes_in = [sig(f"codes_in{b}", 0, step=16) for b in range(2)]
        consts = sig("consts", 0)
        crt = sig("consts_rounded", 0)
        a_exp, a_ready = sig("a_exp", 0), sig("a_ready", 0)
        win_ok, wout_ok = sig("win_split", 0), sig("wout_split", 0)
        win_top, wout_top = sig("win_hi_done", 0), sig("wout_hi_done", 0)
        wsc = sig("wout_scaled", 0)
        cstep = sig("code_step", 0)
        quad = sig("scales_times_four", 0)
        deq = sig("dequantized", 0)
        wt_hi = sig("weights_hi", 0)
        wt_lo = sig("weights_lo", 0)
        u_in = sig("u_in", 1, step=16)
        uT_h, uT_l = sig("uT_hi_done", 2), sig("uT_lo_done", 2)
        dt_exp, dt_step = sig("dt_exp", 1), sig("dt_step", 20)
        dA_ok = sig("dA_split", 1)
        conv0, conv = sig("conv_first_tap", 6), sig("conv_taps", 18)
        x_tanh, z_tanh = sig("x_tanh", 6), sig("z_tanh", 4)
        xbc_ok, zs_ok = sig("xbc_ready", 6), sig("zs_ready", 4)
        R_ok, dec_ok, W_ok = sig("R_ready", 4), sig("decay_ready", 8), sig("W_ready", 4)
        cb_act, cb_ok = sig("cb_scalar_part", 2), sig("cb_ready", 2)
        e2_ok = sig("e2_ready", 2)
        x_ok, xt_ok = sig("xdt_ready", 4), sig("xtail_ready", 2)
        y_step = sig("y_step", 16)
        ssq_ok, rms_step = sig("ssq_ready", 4), sig("rms_step", 12)
        gT_h, gT_l = sig("gT_hi_done", 4), sig("gT_lo_done", 4)
        r_ok, ln_bn, ln_mv, ln_pow, h_ok = (sig("residual", 4), sig("ln_stats", 4), sig("ln_mean_var", 4),
                                            sig("ln_pow", 2), sig("h_ready", 4))
        G_ready, U_ready = sig("gate_ready", 17, 2 * UNITS), sig("up_ready", 17, 2 * UNITS)
        hres_ok = sig("h_res_ready", 1, step=16)
        hT_h, hT_l = sig("hT_hi_done", 2), sig("hT_lo_done", 2)
        gelu_ok, inter_ok = sig("gelu_ready", 16), sig("inter_ready", 16)
        in_h, in_l, down_ok = sig("inter_hi", 16), sig("inter_lo", 16), sig("down_done", 16)
        half_down = sig("first_bank_done", 1)
        o_sum, o_bn, o_mv, o_pow, o_ok = (sig("out_residual", 4), sig("out_stats", 4), sig("out_mean_var", 4),
                                          sig("out_pow", 2), sig("out_ready", 4))
        stored = sig("stored", 1, step=16)

        def bank(use):
            return MB[USES.index(use) % 4]

        def ready(use):
            n = USES.index(use)
            return bank_ready[n % 4], n // 4 + 1

        def wait_ready(eng, use, g):
            s, k = ready(use)
            wait(eng, s, g, k)

        read_by = {"uT0": (uT_l, 1), "uT1": (uT_l, 2), "dt": (dt_step, 2)}
        for n, c in enumerate(CONV_ORDER):
            read_by[f"x{c}"] = (conv, 3 * n + 3)
        for q in range(2):
            read_by[f"CB{q}"], read_by[f"Yoff{q}"] = (e2_ok, q + 1), (y_step, 8 * q + 6)
        for t in range(4):
            read_by |= {f"z{t}": (zs_ok, t + 1), f"XT{t}": (x_ok, t + 1), f"D{t}a": (dec_ok, 2 * t + 1),
                        f"D{t}b": (dec_ok, 2 * t + 2), f"Y{t}": (y_step, (2, 5, 10, 13)[t]),
                        f"gT{t}": (gT_l, t + 1), f"op{t}": (r_ok, t + 1)}

        def wait_bank(eng, use, g):
            n = USES.index(use)
            if n >= 4:
                s, k = read_by[USES[n - 4]]
                wait(eng, s, g, k)
            else:
                s, k = read_by[USES[n::4][-1]]
                wait(eng, s, g - 1, k)

        def f32(ap):
            return ap.bitcast(F32)

        def run(g, last, mixer, ffn, prep=None):
            if prep:
                order = stages("prep", range(2, UNITS + 1), BEFORE_H)
            else:
                order = stages("unit", range(NF), len(SLOTS) - 1)
            for kind, item in order:
                if kind == "mixer":
                    mixer(item, g)
                elif kind == "prep":
                    prep(item)
                else:
                    ffn(kind, item, g - 1)
            if not prep:
                ffn("down", NF - 2, g - 1)
            if not last:
                mixer("uT", g + 1)
            ffn("F1", 0, g)
            if not prep:
                ffn("down", NF - 1, g - 1)
                ffn("final_sum", 0, g - 1)
            if not last:
                mixer("dt", g + 1)
                mixer("x4", g + 1)
                if not prep:
                    ffn("final_norm", 0, g - 1)

        def run_end(ffn):
            for n in range(NF):
                ffn("unit", n, GROUPS - 1)
                if n == 0:
                    ffn("final_norm", 0, GROUPS - 2)
            for n in (NF - 2, NF - 1):
                ffn("down", n, GROUPS - 1)
            ffn("final_sum", 0, GROUPS - 1)
            ffn("final_norm", 0, GROUPS - 1)

        def prep_dst(n, a):
            kind, i = n // 4, n % 4
            if kind < 2:
                return [w[:, a, i * 512:(i + 1) * 512].rearrange("p (q m) -> p q m", q=4)
                        for w in ((wg_hi, wg_lo), (wu_hi, wu_lo))[kind]]
            t0 = 8 * (i % 2) + a
            return [w[:, t0:t0 + 7:2, (i // 2) * P:(i // 2 + 1) * P] for w in (wd_hi, wd_lo)]

        block = ctx.enter_context(nc.Block())

        @block.sync
        def _(sp):
            def load_codes(n):
                if n >= 2:
                    wait(sp, cstep, 0, STEPS * (n - 1))
                kind, i = n // 4, n % 4
                if kind < 2:
                    src = (gate_p, up_p)[kind].rearrange("(b p a) j -> p b (a j)", p=P, a=2)[:, 2 * i:2 * i + 2, :]
                    dst = raw[:, n % 2, :].rearrange("p (b j) -> p b j", b=2)
                else:
                    src = down_p.rearrange("(t p) j -> p t j", p=P)[:, i // 2, (i % 2) * 512:(i % 2) * 512 + 512]
                    dst = raw[:, n % 2, :]
                sp.dma_start(dst, src).then_inc(codes_in[n % 2].sem, 16)

            def load_scales(sc, src, landed):
                sp.dma_start(sc[:, :].rearrange("p (b c) -> p b c", b=NF // 2),
                             src.rearrange("(b p a) c -> p b (a c)", p=P, a=2)).then_inc(landed.sem, 16)

            load_codes(0)
            load_scales(g_sc, gate_s, gsc_in)
            sp.dma_start(rows[0:24, :], conv_w.rearrange("i (c p) -> (i c) p", p=P)).then_inc(rows_in.sem, 16)
            sp.dma_start(rows[24:30, :], conv_b.rearrange("(c p) -> c p", p=P)).then_inc(rows_in.sem, 16)
            sp.dma_start(rows[30:34, :], norm_scale.rearrange("(c p) -> c p", p=P)).then_inc(rows_in.sem, 16)
            sp.dma_start(u_sb[:, :, :], u_v[0]).then_inc(u_in.sem, 16)
            load_codes(1)
            for k in range(KT):
                sp.dma_start(win_raw[:, k, :], W_in[k * P:(k + 1) * P, :]).then_inc(win_in[k].sem, 16)
            for dst, src in ((dtb, dt_bias), (a_neg, A_log), (d_bc, D)):
                sp.dma_start(dst[:, :], src.partition_broadcast(P)).then_inc(small_in.sem, 16)
            load_scales(u_sc, up_s, sc_in)
            sp.dma_start(d_sc[:, :, :], down_s.rearrange("(t p) b -> p t b", p=P)).then_inc(sc_in.sem, 16)
            sp.dma_start(wout_raw, W_out.rearrange("(j p) d -> p j d", p=P)).then_inc(wout_in.sem, 16)
            for n in range(2, UNITS):
                load_codes(n)

            def wait_for(*rises):
                values = [s.at(group, k) for s, group, k in rises]
                values = [v if isinstance(v, int) else sp.to_reg(v) for v in values]
                sp.wait_ge(wout_in.sem, 16)
                for (s, _, _), v in zip(rises, values):
                    sp.wait_ge(s.sem, v)

            def load_u(g):
                wait_for((r_ok, g - 1, 4))
                sp.dma_start(u_sb[:, :, :], u_v[g]).then_inc(u_in.sem, 16)

            def store(f):
                wait_for((o_ok, f, 4))
                sp.dma_start(out_v[f], h_res[:, :, :]).then_inc(stored.sem, 16)

            def keep_h(f):
                wait_for((h_ok, f, 4), *([(stored, f, 0)] if not isinstance(f, int) or f > 0 else []))
                sp.dma_start(h_res[:, :, :], h_sb[:, :, :]).then_inc(hres_ok.sem, 16)

            load_u(1)
            keep_h(0)
            with sp.Fori(1, GROUPS - 1) as g:
                load_u(g + 1)
                store(g - 1)
                keep_h(g)
            store(GROUPS - 2)
            keep_h(GROUPS - 1)
            store(GROUPS - 1)
            wait(sp, stored, GROUPS - 1, 1)

        @block.tensor
        def _(pe):
            def mm3(dst, left, right, first, last):
                (lh, ll), (rh, rl) = left, right
                nc.tensor.matmul(dst, lh, rh, start=first, stop=False, skip_group_check=True)
                nc.tensor.matmul(dst, lh, rl, start=False, stop=False, skip_group_check=True)
                return nc.tensor.matmul(dst, ll, rh, start=False, stop=last, skip_group_check=True)

            def dt_product(t):
                c = 2 * H * t
                for k in range(KT):
                    nc.tensor.matmul(bank("dt")[:, c:c + 2 * H], uT_hi[:, k, t * P:(t + 1) * P],
                                     wdt[:, k, :, :].rearrange("p a h -> p (a h)"), start=k == 0, stop=False,
                                     skip_group_check=True)
                    mm = nc.tensor.matmul(bank("dt")[:, c:c + H], uT_lo[:, k, t * P:(t + 1) * P], wdt[:, k, 0, :],
                                          start=False, stop=k == KT - 1, skip_group_check=True)
                return mm

            def mixer(name, g):
                kind, i = split_name(name)
                if kind == "uT":
                    wait(pe, u_in, g, 1)
                    for k in range(KT):
                        use = f"uT{k}"
                        wait_bank(pe, use, g)
                        for t in range(NT):
                            mm = nc.tensor.transpose(bank(use)[:, t * P:(t + 1) * P],
                                                     u_sb[:, t, k * P:(k + 1) * P], ident[:, :])
                        mm.then_inc(ready(use)[0].sem, 1)
                elif kind == "x":
                    if i == 4:
                        wait(pe, uT_l, g, 2)
                        wait_bank(pe, "dt", g)
                    use, c0 = f"x{i}", X0 + i * P
                    wait_bank(pe, use, g)
                    for k in range(KT):
                        mm = mm3(bank(use)[:, :], [w[:, k, c0:c0 + P] for w in (win_hi, win_lo)],
                                 [x[:, k, :] for x in (uT_hi, uT_lo)], k == 0, k == KT - 1)
                        if i == 4:
                            dt_product(2 * k)
                            dt_mm = dt_product(2 * k + 1)
                    mm.then_inc(ready(use)[0].sem, 1)
                    if i == 4:
                        dt_mm.then_inc(ready("dt")[0].sem, 1)
                elif kind == "z":
                    use = f"z{i}"
                    wait_bank(pe, use, g)
                    for k in range(KT):
                        mm = mm3(bank(use)[:, :], [x[:, k, i * P:(i + 1) * P] for x in (uT_hi, uT_lo)],
                                 [w[:, k, 0:DI] for w in (win_hi, win_lo)], k == 0, k == KT - 1)
                    mm.then_inc(ready(use)[0].sem, 1)
                elif kind == "CB":
                    use, s = f"CB{i}", i * SEQ
                    wait_bank(pe, use, g)
                    wait(pe, xbc_ok, g, 6)
                    wait(pe, dA_ok, g, 1)
                    b = bank(use)
                    nc.tensor.matmul(b[:, 0:2 * P], xbc[:, 4, s:s + P], xbc[:, 5, s:s + 2 * P],
                                     start=True, stop=True)
                    nc.tensor.matmul(b[:, 2 * P:3 * P], xbc[:, 4, s + P:s + 2 * P], xbc[:, 5, s + P:s + 2 * P],
                                     start=True, stop=True)
                    nc.tensor.matmul(b[:, 3 * P:3 * P + H], tri_r[:, :], dA_hi[:, 2 * i + 1, :],
                                     start=True, stop=False)
                    nc.tensor.matmul(b[:, 3 * P:3 * P + H], tri_r[:, :], dA_lo[:, 2 * i + 1, :],
                                     start=False, stop=True).then_inc(ready(use)[0].sem, 1)
                elif kind == "XT":
                    use = f"XT{i}"
                    wait_bank(pe, use, g)
                    for j in range(JT):
                        mm = nc.tensor.transpose(bank(use)[:, j * P:(j + 1) * P],
                                                 xbc[:, j, i * P:(i + 1) * P], ident[:, :])
                    mm.then_inc(ready(use)[0].sem, 1)
                elif kind == "D":
                    wait(pe, R_ok, g, i + 1)
                    for n, use in enumerate((f"D{i}a", f"D{i}b")):
                        wait_bank(pe, use, g)
                        hs = slice(4 * n, 4 * n + 4)
                        nc.tensor.matmul(bank(use)[:, :], after_r[:, :], R_hi[:, hs, :], start=True, stop=False)
                        nc.tensor.matmul(bank(use)[:, :], after_r[:, :], R_lo[:, hs, :], start=False,
                                         stop=True).then_inc(ready(use)[0].sem, 1)
                elif kind == "Y":
                    use = f"Y{i}"
                    wait_bank(pe, use, g)
                    wait(pe, x_ok, g, i + 1)
                    wait(pe, W_ok, g, i + 1)
                    for h in range(H):
                        mm = nc.tensor.matmul(bank(use)[:, h * HP:(h + 1) * HP], dec[:, h, :],
                                              xdt[:, h * HP:(h + 1) * HP], start=True, stop=True)
                    mm.then_inc(ready(use)[0].sem, 1)
                    if i % 2:
                        use = f"Yoff{i // 2}"
                        wait_bank(pe, use, g)
                        wait(pe, xt_ok, g, i // 2 + 1)
                        nc.tensor.matmul(bank(use)[:, :], cb[:, 1, :], xtail[:, :], start=True,
                                         stop=True).then_inc(ready(use)[0].sem, 1)
                elif kind == "gT":
                    use = f"gT{i}"
                    wait_bank(pe, use, g)
                    wait(pe, y_step, g, (3, 8, 11, 16)[i])
                    for j in range(JT):
                        mm = nc.tensor.transpose(bank(use)[:, j * P:(j + 1) * P],
                                                 zs[:, i, j * P:(j + 1) * P], ident[:, :])
                    mm.then_inc(ready(use)[0].sem, 1)
                elif kind == "op":
                    use = f"op{i}"
                    wait_bank(pe, use, g)
                    wait(pe, gT_l, g, i + 1)
                    for j in range(JT):
                        mm = mm3(bank(use)[:, 0:DM], [x[:, j * P:(j + 1) * P] for x in (gT_hi, gT_lo)],
                                 [w[:, j, :] for w in (wout_hi, wout_lo)], j == 0, j == JT - 1)
                    mm.then_inc(ready(use)[0].sem, 1)

            def down(n, f):
                wait(pe, in_l, f, n + 1)
                for t in range(NT):
                    mm = mm3(OB[t // 2][:, (t % 2) * DM:(t % 2 + 1) * DM],
                             [x[:, n % 2, t * P:(t + 1) * P] for x in (in_hi, in_lo)],
                             [w[:, n, :] for w in (wd_hi, wd_lo)], n == 0 and t % 2 == 0, n == NF - 1)
                    if n == NF - 1 and t == 1:
                        mm.then_inc(half_down.sem, 1)
                mm.then_inc(down_ok.sem, 1)

            def ffn(kind, n, f):
                if kind == "F1":
                    wait(pe, h_ok, f, 4)
                    if isinstance(f, int) and f == 0:
                        pe.wait_ge(wt_lo.sem, 2 * UNITS)
                    else:
                        wait(pe, gelu_ok, f - 1, NF)
                        wait(pe, inter_ok, f - 1, NF)
                    for k, (b, done) in enumerate(((GB, G_ready), (UB, U_ready))):
                        for t in range(NT):
                            mm = nc.tensor.transpose(b[:, t * P:(t + 1) * P], h_sb[:, t, k::2], ident[:, :])
                        mm.then_inc(done.sem, 1)
                elif kind == "unit":
                    if n == 0:
                        wait(pe, hT_l, f, 2)
                    for wh, wl, b, done, read in ((wg_hi, wg_lo, GB, G_ready, gelu_ok),
                                                  (wu_hi, wu_lo, UB, U_ready, inter_ok)):
                        if n:
                            wait(pe, read, f, n)
                        for k in range(KT):
                            mm = mm3(b[:, :], [w[:, k, n * P:(n + 1) * P] for w in (wh, wl)],
                                     [x[:, k, :] for x in (hT_hi, hT_lo)], k == 0, k == KT - 1)
                        mm.then_inc(done.sem, 1)
                    if n >= 2:
                        down(n - 2, f)
                elif kind == "down":
                    down(n, f)

            def first_mixer(name, g):
                if name == "op0":
                    pe.wait_ge(wout_ok.sem, 1)
                mixer(name, g)

            def prep(step):
                n = step - 1
                if n < 0:
                    return
                wait(pe, deq, 0, 2 * n + 2)
                for a, (b, done) in enumerate(((GB, G_ready), (UB, U_ready))):
                    if n:
                        pe.wait_ge(wt_lo.sem, 2 * n - 1 + a)
                    for q in range(4):
                        mm = nc.tensor.matmul(b[:, q * P:(q + 1) * P], wdq[:, a, q * P:(q + 1) * P], ident[:, :],
                                              start=q == 0, stop=False, skip_group_check=True)
                    mm.then_inc(done.sem, 1)
                for a, (b, done) in enumerate(((GB, G_ready), (UB, U_ready))):
                    pe.wait_ge(wt_hi.sem, 2 * n + a + 1)
                    nc.tensor.matmul(b[:, :], minus_ident_r[:, :], prep_dst(n, a)[0], start=False, stop=True,
                                     skip_group_check=True).then_inc(done.sem, 1)

            pe.wait_ge(consts.sem, 5)
            pe.wait_ge(rows_in.sem, 16 * 3)
            nc.tensor.transpose(MB[0][:, 0:34], rows, ident[0:34, 0:34]).then_inc(bank_ready[0].sem, 1)
            pe.wait_ge(crt.sem, 5)
            mixer("uT", 0)
            prep(1)
            pe.wait_ge(win_ok.sem, 3)
            mixer("x4", 0)
            run(0, False, first_mixer, ffn, prep)
            with pe.Fori(1, GROUPS - 1) as g:
                run(g, False, mixer, ffn)
            run(GROUPS - 1, True, mixer, ffn)
            run_end(ffn)

        @block.scalar
        def _(act):
            def tanh(n, g):
                c = CONV_ORDER[n]
                wait(act, conv, g, 3 * n + 3)
                wait(act, ssq_ok, g - 1, NT)
                if n >= 2:
                    wait(act, xbc_ok, g, n - 1)
                nc.scalar.activation(y[:, n % 2, :], xbc[:, c, :], ACT.Tanh).then_inc(x_tanh.sem, 1)

            def mixer(name, g):
                kind, i = split_name(name)
                if kind == "uT":
                    wait_ready(act, "D3b", g - 1)
                    for k in range(KT):
                        wait_ready(act, f"uT{k}", g)
                        nc.scalar.activation(uT_hi[:, k, :], bank(f"uT{k}")[:, :], ACT.Copy).then_inc(uT_h.sem, 1)
                elif kind == "x":
                    n = CONV_ORDER.index(i)
                    wait_ready(act, f"x{i}", g)
                    wait_ready(act, "XT3", g - 1)
                    nc.scalar.activation(xbc[:, i, :], bank(f"x{i}")[:, :], ACT.Identity,
                                         bias=chan[:, 24 + i:25 + i],
                                         scale=chan[:, 18 + i:19 + i]).then_inc(conv0.sem, 1)
                    if n == 0:
                        wait(act, dt_step, g, 3)
                        nc.scalar.activation(dte[:, :], dte[:, :], ACT.Exp).then_inc(dt_exp.sem, 1)
                    for m in (() if n < 2 else (0, 1) if n == 2 else (n - 1,)):
                        tanh(m, g)
                elif kind == "z":
                    if i == NT - 1:
                        tanh(CT - 1, g)
                    wait_ready(act, f"z{i}", g)
                    wait_ready(act, f"gT{i}", g - 1)
                    wait(act, ssq_ok, g - 1, i + 1)
                    nc.scalar.activation(zs[:, i, :], bank(f"z{i}")[:, :], ACT.Tanh, scale=0.5)\
                        .then_inc(z_tanh.sem, 1)
                elif kind == "CB":
                    wait_ready(act, f"CB{i}", g)
                    if i:
                        wait_ready(act, "Yoff0", g)
                    else:
                        wait_ready(act, "Yoff1", g - 1)
                    nc.scalar.activation(cb[:, 1, :], bank(f"CB{i}")[:, P:2 * P], ACT.Copy).then_inc(cb_act.sem, 1)
                elif kind == "D":
                    if i % 2 == 0:
                        wait(act, cb_ok, g, i // 2 + 1)
                        nc.scalar.activation(e2[:, i // 2, :], bank(f"CB{i // 2}")[:, 3 * P:3 * P + H],
                                             ACT.Exp).then_inc(e2_ok.sem, 1)
                    if i:
                        wait_ready(act, f"Y{i - 1}", g)
                    else:
                        wait_ready(act, "Y3", g - 1)
                    for n, use in enumerate((f"D{i}a", f"D{i}b")):
                        wait_ready(act, use, g)
                        nc.scalar.activation(dec[:, 4 * n:4 * n + 4, :],
                                             bank(use)[:, :].rearrange("p (h l) -> p h l", h=4),
                                             ACT.Exp).then_inc(dec_ok.sem, 1)
                elif kind == "gT":
                    wait(act, y_step, g, (3, 8, 11, 16)[i])
                    nc.scalar.activation(y[:, i % 2, :], zs[:, i, :], ACT.Square,
                                         accum_out=ssq[:, i:i + 1]).then_inc(ssq_ok.sem, 1)
                    wait_ready(act, f"gT{i}", g)
                    if i:
                        wait_ready(act, f"op{i - 1}", g)
                    else:
                        wait_ready(act, "op3", g - 1)
                    nc.scalar.activation(gT_hi[:, :], bank(f"gT{i}")[:, :], ACT.Copy).then_inc(gT_h.sem, 1)

            def inter_hi(n, f):
                wait(act, inter_ok, f, n + 1)
                if n >= 2:
                    wait(act, down_ok, f, n - 1)
                nc.scalar.activation(in_hi[:, n % 2, :], act_sb[:, n % 2, :], ACT.Copy).then_inc(in_h.sem, 1)

            def ffn(kind, n, f):
                if kind == "F1":
                    for k, (b, done) in enumerate(((GB, G_ready), (UB, U_ready))):
                        wait(act, done, f, 1)
                        nc.scalar.activation(hT_hi[:, k, :], b[:, :], ACT.Copy).then_inc(hT_h.sem, 1)
                elif kind == "unit":
                    if n:
                        inter_hi(n - 1, f)
                    wait(act, G_ready, f, n + 2)
                    if n >= 2:
                        wait(act, in_l, f, n - 1)
                    nc.scalar.activation(act_sb[:, n % 2, :], GB[:, :], ACT.Gelu_apprx_tanh).then_inc(gelu_ok.sem, 1)
                elif kind == "down" and n == NF - 2:
                    inter_hi(NF - 1, f)

            def prep(step):
                n = step - 1
                if n < 0:
                    return
                for part, signal in ((0, wt_hi), (1, wt_lo)):
                    for a, (b, done) in enumerate(((GB, G_ready), (UB, U_ready))):
                        act.wait_ge(done.sem, 2 * n + 1 + part)
                        nc.scalar.activation(prep_dst(n, a)[part], b[:, :].rearrange("p (q m) -> p q m", q=4),
                                             ACT.Copy).then_inc(signal.sem, 1)

            def first_mixer(name, g):
                if name == "x1":
                    act.wait_ge(wsc.sem, 4)
                    nc.scalar.activation(wout_hi[:, :, :], wout_raw, ACT.Copy).then_inc(wout_top.sem, 1)
                if name == "z2":
                    act.wait_ge(wout_ok.sem, 1)
                mixer(name, g)

            for k in range(KT):
                act.wait_ge(win_in[k].sem, 16)
                nc.scalar.activation(win_hi[:, k, :], win_raw[:, k, :], ACT.Copy).then_inc(win_top.sem, 1)
            nc.scalar.activation(wdt[:, :, 0, :], win_raw[:, :, DT0:NIN], ACT.Copy).then_inc(win_top.sem, 1)
            mixer("uT", 0)
            act.wait_ge(small_in.sem, 16 * 3)
            nc.scalar.activation(a_neg[:, :], a_neg[:, :], ACT.Exp).then_inc(a_exp.sem, 1)
            prep(1)
            act.wait_ge(crt.sem, 5)
            act.wait_ge(win_ok.sem, 3)
            mixer("x4", 0)
            run(0, False, first_mixer, ffn, prep)
            with act.Fori(1, GROUPS - 1) as g:
                run(g, False, mixer, ffn)
            run(GROUPS - 1, True, mixer, ffn)
            run_end(ffn)

        @block.vector
        def _(dve):
            tt, ts, stt = nc.vector.tensor_tensor, nc.vector.tensor_scalar, nc.vector.scalar_tensor_tensor

            def head(ap):
                return ap.rearrange("p (h c) -> p h c", h=H)

            def silu(n, g):
                c = CONV_ORDER[n]
                wait(dve, x_tanh, g, n + 1)
                stt(xbc[:, c, :], y[:, n % 2, :], 1.0, xbc[:, c, :], ALU.add, ALU.mult).then_inc(xbc_ok.sem, 1)

            def dt_chain(k, g):
                if k:
                    wait(dve, dt_step, g, k)
                flat = dt_sb[:, :, :].rearrange("p t h -> p (t h)")
                by_head = dtx[:, :].rearrange("p (t h) -> p t h", t=NT)
                parts = bank("dt")[:, 0:2 * NT * H].rearrange("p (t h) -> p t h", t=NT)
                if k == 0:
                    wait_ready(dve, "dt", g)
                    ins = tt(by_head, parts[:, :, 0:H], dtb[:, :].unsqueeze(1).to_broadcast([P, NT, H]), ALU.add)
                elif k == 1:
                    ins = tt(by_head, parts[:, :, H:2 * H], by_head, ALU.add)
                elif k == 2:
                    ins = stt(dte[:, :], dtx[:, :], -1.0, dtx[:, :], ALU.mult, ALU.min)
                elif k == 3:
                    ins = ts(dtx[:, :], dtx[:, :], 0.0, None, ALU.max)
                elif k == 4:
                    wait(dve, dt_exp, g, 1)
                    ins = ts(dtp[:, :], dte[:, :], 2.0, None, ALU.add)
                elif k == 5:
                    ins = nc.vector.reciprocal(dtp[:, :], dtp[:, :])
                elif k == 6:
                    ins = tt(dts[:, :], dte[:, :], dtp[:, :], ALU.mult)
                elif k == 7:
                    ins = tt(dtq[:, :], dts[:, :], dts[:, :], ALU.mult)
                elif k == 8:
                    ins = ts(dtp[:, :], dtq[:, :], 1.0 / 17, None, ALU.mult)
                elif k <= 15:
                    ins = stt(dtp[:, :], dtp[:, :], 1.0 / (33 - 2 * k), dtq[:, :], ALU.add, ALU.mult)
                elif k == 16:
                    ins = stt(dtp[:, :], dtp[:, :], 1.0, dts[:, :], ALU.add, ALU.mult)
                elif k == 17:
                    ins = stt(flat, dtp[:, :], 2.0, dtx[:, :], ALU.mult, ALU.add)
                elif k == 18:
                    ins = tt(dA[:, :, :], dt_sb[:, :, :], a_neg[:, :].unsqueeze(1).to_broadcast([P, NT, H]),
                             ALU.mult)
                elif k == 19:
                    ins = nc.vector.tensor_copy(dA_hi[:, :, :], dA[:, :, :])
                else:
                    ins = tt(dA_lo[:, :, :], dA[:, :, :], f32(dA_hi[:, :, :]), ALU.subtract)
                ins.then_inc(dA_ok.sem if k == 20 else dt_step.sem, 1)

            def mixer(name, g):
                kind, i = split_name(name)
                if kind == "uT":
                    for k in range(KT):
                        wait(dve, uT_h, g, k + 1)
                        tt(uT_lo[:, k, :], bank(f"uT{k}")[:, :], f32(uT_hi[:, k, :]), ALU.subtract)\
                            .then_inc(uT_l.sem, 1)
                elif kind == "dt":
                    for k in range(3):
                        dt_chain(k, g)
                elif kind == "x":
                    n = CONV_ORDER.index(i)
                    acc = xbc[:, i, :].rearrange("p (q s) -> p q s", q=2)
                    src = bank(f"x{i}")[:, :].rearrange("p (q s) -> p q s", q=2)
                    wait(dve, conv0, g, n + 1)
                    for d in (1, 2, 3):
                        c = (3 - d) * CT + i
                        ins = stt(acc[:, :, d:], src[:, :, 0:SEQ - d], chan[:, c:c + 1], acc[:, :, d:],
                                  ALU.mult, ALU.add)
                        ins.then_inc(conv.sem, 1)
                        if i < JT:
                            dt_chain(4 * i + d + 2, g)
                        wait(dve, conv, g, 3 * n + d)
                    for m in (() if n < 2 else (0, 1) if n == 2 else (n - 1,)):
                        silu(m, g)
                elif kind == "z":
                    if i == NT - 1:
                        dt_chain(18, g)
                        silu(CT - 1, g)
                        dt_chain(19, g)
                    wait(dve, z_tanh, g, i + 1)
                    stt(zs[:, i, :], zs[:, i, :], 1.0, bank(f"z{i}")[:, :], ALU.add, ALU.mult)\
                        .then_inc(zs_ok.sem, 1)
                    dt_chain(4 * i + 6 if i < NT - 1 else 20, g)
                elif kind == "CB":
                    wait(dve, cb_act, g, i + 1)
                    tt(cb[:, 0, :], bank(f"CB{i}")[:, 0:P], tri[:, :], ALU.mult)
                    tt(cb[:, 2, :], bank(f"CB{i}")[:, 2 * P:3 * P], tri[:, :], ALU.mult).then_inc(cb_ok.sem, 1)
                elif kind == "XT":
                    use = f"XT{i}"
                    wait_ready(dve, use, g)
                    wait(dve, ssq_ok, g, i - 1)
                    tt(head(y[:, i % 2, :]), head(bank(use)[:, :]),
                       d_bc[:, :].unsqueeze(2).to_broadcast([P, H, HP]), ALU.mult).then_inc(y_step.sem, 1)
                    tt(head(xdt[:, :]), head(bank(use)[:, :]),
                       dt_sb[:, i, :].unsqueeze(2).to_broadcast([P, H, HP]), ALU.mult).then_inc(x_ok.sem, 1)
                elif kind == "D":
                    wait(dve, dec_ok, g, 2 * i + 2)
                    if i % 2 == 0:
                        wait(dve, x_ok, g, i + 1)
                        tt(head(xtail[:, :]), head(xdt[:, :]), dec[:, :, P - 1:P].to_broadcast([P, H, HP]),
                           ALU.mult).then_inc(xt_ok.sem, 1)
                        wait(dve, xt_ok, g, i // 2 + 1)
                    wait(dve, cb_ok, g, i // 2 + 1)
                    tt(dec[:, :, :], dec[:, :, :], cb[:, 2 * (i % 2):2 * (i % 2) + 1, :].to_broadcast([P, H, P]),
                       ALU.mult).then_inc(W_ok.sem, 1)
                elif kind == "Y":
                    s0 = (0, 3, 8, 11)[i]
                    yc = y[:, i % 2, :]
                    wait_ready(dve, f"Y{i}", g)
                    wait(dve, y_step, g, s0 + 1)
                    tt(yc, bank(f"Y{i}")[:, :], yc, ALU.add).then_inc(y_step.sem, 1)
                    wait(dve, y_step, g, s0 + 2)
                    s0 += 2
                    if i % 2:
                        use = f"Yoff{i // 2}"
                        wait_ready(dve, use, g)
                        wait(dve, e2_ok, g, i // 2 + 1)
                        tt(head(xdt[:, :]), head(bank(use)[:, :]),
                           e2[:, i // 2, :].unsqueeze(2).to_broadcast([P, H, HP]), ALU.mult)\
                            .then_inc(y_step.sem, 1)
                        wait(dve, y_step, g, s0 + 1)
                        tt(yc, yc, xdt[:, :], ALU.add).then_inc(y_step.sem, 1)
                        wait(dve, y_step, g, s0 + 2)
                    wait(dve, zs_ok, g, i + 1)
                    tt(zs[:, i, :], zs[:, i, :], yc, ALU.mult).then_inc(y_step.sem, 1)
                elif kind == "gT":
                    wait(dve, gT_h, g, i + 1)
                    tt(gT_lo[:, :], bank(f"gT{i}")[:, :], f32(gT_hi[:, :]), ALU.subtract).then_inc(gT_l.sem, 1)
                elif kind == "op":
                    if i == 0:
                        wait(dve, hres_ok, g, 0)
                    wait_ready(dve, f"op{i}", g)
                    wait(dve, rms_step, g, 3 * i + 3)
                    stt(h_sb[:, i, :], bank(f"op{i}")[:, 0:DM], rms[:, i:i + 1], u_sb[:, i, :],
                        ALU.mult, ALU.add).then_inc(r_ok.sem, 1)
                elif name == "ln1":
                    norm_stats(h_sb, bn6, mv, (r_ok, ln_bn, ln_mv), g)
                elif name == "ln2":
                    norm_apply(h_sb, mv, lnr, (ln_mv, ln_pow, h_ok), g)

            def norm_stats(x, six, two, signals, g):
                summed, stats, moments = signals
                for t in range(NT):
                    wait(dve, summed, g, t + 1)
                    nc.vector.bn_stats(six[:, t, :], x[:, t, :]).then_inc(stats.sem, 1)
                for t in range(NT):
                    dve.wait_ge(consts.sem, 5)
                    wait(dve, stats, g, t + 1)
                    nc.vector.bn_aggr(two[:, t, :], six[:, t, :]).then_inc(moments.sem, 1)

            def norm_apply(x, two, rs, signals, g):
                moments, power, done = signals
                wait(dve, moments, g, 4)
                wait(dve, power, g, 2)
                for t in range(NT):
                    ts(x[:, t, :], x[:, t, :], two[:, t, 0:1], rs[:, t:t + 1], ALU.subtract, ALU.mult)\
                        .then_inc(done.sem, 1)

            def inter_lo(n, f):
                wait(dve, in_h, f, n + 1)
                tt(in_lo[:, n % 2, :], act_sb[:, n % 2, :], f32(in_hi[:, n % 2, :]), ALU.subtract)\
                    .then_inc(in_l.sem, 1)

            def ffn(kind, n, f):
                if kind == "F1":
                    for k, b in enumerate((GB, UB)):
                        wait(dve, hT_h, f, k + 1)
                        tt(hT_lo[:, k, :], b[:, :], f32(hT_hi[:, k, :]), ALU.subtract).then_inc(hT_l.sem, 1)
                elif kind == "unit":
                    if n:
                        inter_lo(n - 1, f)
                    wait(dve, gelu_ok, f, n + 1)
                    wait(dve, U_ready, f, n + 2)
                    tt(act_sb[:, n % 2, :], UB[:, :], act_sb[:, n % 2, :], ALU.mult).then_inc(inter_ok.sem, 1)
                elif kind == "down" and n == NF - 2:
                    inter_lo(NF - 1, f)
                elif kind == "final_sum":
                    wait(dve, hres_ok, f, 1)
                    for t in range(NT):
                        if t == 0:
                            wait(dve, half_down, f, 1)
                        if t == 2:
                            wait(dve, down_ok, f, NF)
                        tt(h_res[:, t, :], OB[t // 2][:, (t % 2) * DM:(t % 2 + 1) * DM], h_res[:, t, :],
                           ALU.add).then_inc(o_sum.sem, 1)
                    norm_stats(h_res, fbn6, fmv, (o_sum, o_bn, o_mv), f)
                elif kind == "final_norm":
                    norm_apply(h_res, fmv, flnr, (o_mv, o_pow, o_ok), f)

            def prep(n):
                if n >= UNITS:
                    return
                word = raw[:, n % 2, :]
                s0 = STEPS * n
                dve.wait_ge(codes_in[n % 2].sem, 16 * (n // 2 + 1))
                ts(word, raw8[:, n % 2, :], float(SPREAD), None, ALU.mult).then_inc(cstep.sem, 1)
                if n:
                    wait(dve, deq, 0, 2 * n)
                wait(dve, cstep, 0, s0 + 1)
                ts(code, word, MAGNITUDES, QUARTER_BITS * (1 + 2**16), ALU.bitwise_and, ALU.bitwise_or)\
                    .then_inc(cstep.sem, 1)
                wait(dve, cstep, 0, s0 + 2)
                ts(other.bitcast(BF16), code.bitcast(BF16), 2.0, -0.25, ALU.mult, ALU.add).then_inc(cstep.sem, 1)
                ts(word, word, 6, SIGNS, ALU.logical_shift_left, ALU.bitwise_and).then_inc(cstep.sem, 1)
                wait(dve, cstep, 0, s0 + 3)
                tt(code.bitcast(BF16), code.bitcast(BF16), other.bitcast(BF16), ALU.min).then_inc(cstep.sem, 1)
                wait(dve, cstep, 0, s0 + 5)
                tt(code, code, word, ALU.bitwise_or).then_inc(cstep.sem, 1)

            def first_mixer(name, g):
                if name == "x0":
                    dve.wait_ge(wout_in.sem, 16)
                    for j in range(JT):
                        ts(wout_raw[:, j, :], wout_raw[:, j, :], chan[:, 30 + j:31 + j], None, ALU.mult)\
                            .then_inc(wsc.sem, 1)
                if name == "x2":
                    dve.wait_ge(wout_top.sem, 1)
                    tt(wout_lo[:, :, :], wout_raw, f32(wout_hi[:, :, :]), ALU.subtract).then_inc(wout_ok.sem, 1)
                if name == "op0":
                    dve.wait_ge(U_ready.sem, 2 * UNITS - 1)
                mixer(name, g)

            dve.wait_ge(consts.sem, 5)
            nc.vector.tensor_copy(tri_r[:, :], tri[:, :]).then_inc(crt.sem, 1)
            ts(after_r[:, :], tri[:, :], -1.0, 1.0, ALU.mult, ALU.add).then_inc(crt.sem, 1)
            ts(minus_ident_r[:, :], ident[:, :], -1.0, None, ALU.mult).then_inc(crt.sem, 1)
            prep(0)
            dve.wait_ge(bank_ready[0].sem, 1)
            ts(chan[:, 0:30], MB[0][:, 0:30], 0.5, None, ALU.mult).then_inc(crt.sem, 1)
            nc.vector.tensor_copy(chan[:, 30:34], MB[0][:, 30:34]).then_inc(crt.sem, 1)
            dve.wait_ge(crt.sem, 5)
            prep(1)
            for k in range(KT):
                dve.wait_ge(win_top.sem, k + 1)
                tt(win_lo[:, k, :], win_raw[:, k, :], f32(win_hi[:, k, :]), ALU.subtract).then_inc(win_ok.sem, 1)
            dve.wait_ge(win_top.sem, 3)
            tt(wdt[:, :, 1, :], win_raw[:, :, DT0:NIN], f32(wdt[:, :, 0, :]), ALU.subtract).then_inc(win_ok.sem, 1)
            mixer("uT", 0)
            dve.wait_ge(a_exp.sem, 1)
            ts(a_neg[:, :], a_neg[:, :], -1.0, None, ALU.mult).then_inc(a_ready.sem, 1)
            dve.wait_ge(a_ready.sem, 1)
            prep(2)
            mixer("dt", 0)
            mixer("x4", 0)
            run(0, False, first_mixer, ffn, lambda n: prep(n + 1))
            with dve.Fori(1, GROUPS - 1) as g:
                run(g, False, mixer, ffn)
            run(GROUPS - 1, True, mixer, ffn)
            run_end(ffn)

        @block.gpsimd
        def _(pool):
            tt, ts = nc.gpsimd.tensor_tensor, nc.gpsimd.tensor_scalar

            def rsqrt(dst, tmp, var, least, signal, g, k, n):
                tt(tmp, var, least, ALU.add).then_inc(signal.sem, 1)
                wait(pool, signal, g, k)
                tt(dst, tmp, half[:, 0:n], ALU.pow).then_inc(signal.sem, 1)

            def mixer(name, g):
                kind, i = split_name(name)
                if kind == "R":
                    if i:
                        wait_ready(pool, f"D{i - 1}b", g)
                    else:
                        wait_ready(pool, "z3", g)
                    wait(pool, dA_ok, g, 1)
                    mask = tri[:, :].unsqueeze(1).to_broadcast([P, H, P])
                    for R, step in ((R_hi, dA_hi), (R_lo, dA_lo)):
                        ins = tt(R, mask, f32(step[:, i, :]).unsqueeze(2).to_broadcast([P, H, P]), ALU.mult)
                    ins.then_inc(R_ok.sem, 1)
                elif kind == "gT":
                    wait(pool, ssq_ok, g, i + 1)
                    tt(ms[:, i:i + 1], ssq[:, i:i + 1], inv_di[:, :], ALU.mult).then_inc(rms_step.sem, 1)
                    wait(pool, rms_step, g, 3 * i + 1)
                    rsqrt(rms[:, i:i + 1], rms_v[:, i:i + 1], ms[:, i:i + 1], eps4[:, :], rms_step, g,
                          3 * i + 2, 1)
                elif name == "ln1":
                    wait(pool, ln_mv, g, 4)
                    rsqrt(lnr[:, :], lnv[:, :], mv[:, :, 1], eps[:, :], ln_pow, g, 1, NT)

            def ffn(kind, n, f):
                if kind == "final_sum":
                    wait(pool, o_mv, f, 4)
                    rsqrt(flnr[:, :], flnv[:, :], fmv[:, :, 1], eps[:, :], o_pow, f, 1, NT)

            def prep(n):
                if n == UNITS:
                    return
                sc = (g_sc[:, (n % 4) * 32:(n % 4 + 1) * 32], u_sc[:, (n % 4) * 32:(n % 4 + 1) * 32],
                      d_sc[:, (n % 4) // 2, (n % 2) * 32:(n % 2 + 1) * 32])[n // 4]
                wait(pool, cstep, 0, STEPS * (n + 1))
                if n:
                    pool.wait_ge(U_ready.sem, 2 * n - 1)
                for a in range(2):
                    tt(wdq[:, a, :].rearrange("p (b k) -> p b k", b=32),
                       code.bitcast(BF16).rearrange("p (b k a) -> p a b k", b=32, a=2)[:, a, :, :],
                       sc.unsqueeze(2).to_broadcast([P, 32, 16]), ALU.mult).then_inc(deq.sem, 1)

            nc.gpsimd.memset(ident[:, :], 0.0).then_inc(consts.sem, 1)
            nc.gpsimd.memset(tri[:, :], 1.0).then_inc(consts.sem, 1)
            nc.gpsimd.memset(half[:, :], -0.5)
            nc.gpsimd.memset(eps[:, :], EPS)
            nc.gpsimd.memset(eps4[:, :], 4 * EPS)
            nc.gpsimd.memset(inv_di[:, :], 1.0 / DI).then_inc(consts.sem, 1)
            pool.wait_ge(consts.sem, 3)
            nc.gpsimd.affine_select(out=ident[:, :], in_=ident[:, :], compare_op=ALU.not_equal, fill=1.0, base=0,
                                    pattern=[[-1, P]], channel_multiplier=1).then_inc(consts.sem, 1)
            nc.gpsimd.affine_select(out=tri[:, :], in_=tri[:, :], compare_op=ALU.is_ge, fill=0.0, base=0,
                                    pattern=[[1, P]], channel_multiplier=-1).then_inc(consts.sem, 1)
            pool.wait_ge(consts.sem, 5)
            pool.wait_ge(gsc_in.sem, 16)
            ts(g_sc[:, :], g_sc[:, :], 4.0, None, ALU.mult).then_inc(quad.sem, 1)
            pool.wait_ge(quad.sem, 1)
            prep(0)
            pool.wait_ge(sc_in.sem, 16 * 2)
            for sc in (u_sc[:, :], d_sc[:, :, :]):
                ts(sc, sc, 4.0, None, ALU.mult).then_inc(quad.sem, 1)
            pool.wait_ge(quad.sem, 3)
            prep(1)
            run(0, False, mixer, ffn, prep)
            with pool.Fori(1, GROUPS - 1) as g:
                run(g, False, mixer, ffn)
            run(GROUPS - 1, True, mixer, ffn)
            run_end(ffn)


_INS = ["L0_attn_u", "L0_attn_W_in", "L0_attn_conv_w", "L0_attn_conv_b", "L0_attn_dt_bias", "L0_attn_A_log",
        "L0_attn_D", "L0_attn_norm_scale", "L0_attn_W_out", "L0_ffn_gate_W_packed", "L0_ffn_gate_scales",
        "L0_ffn_up_W_packed", "L0_ffn_up_scales", "L0_ffn_down_W_packed", "L0_ffn_down_scales"]
_OUTS = [((16, 256, 256), "float32")]


def kernel(**inputs):
    import numpy as _np
    import concourse.bacc as _bacc
    from concourse import mybir as _mybir
    from concourse.bass_utils import run_bass_kernel_spmd as _run

    nc = _bacc.Bacc("TRN2", target_bir_lowering=False, num_devices=1)
    arrays, args = {}, []
    for name in _INS:
        a = _np.ascontiguousarray(inputs[name])
        arrays[f"in_{name}_dram"] = a
        args.append(nc.dram_tensor(f"in_{name}_dram", a.shape, _mybir.dt.from_np(a.dtype), kind="ExternalInput").ap())
    for i, (shape, dtype) in enumerate(_OUTS):
        dt = _mybir.dt.from_np(_np.dtype(dtype))
        args.append(nc.dram_tensor(f"out_{i}_dram", shape, dt, kind="ExternalOutput").ap())
    mamba_ffn_kernel(nc, *args)
    r = _run(nc, [arrays], core_ids=[0])
    got = tuple(r.results[0][f"out_{i}_dram"] for i in range(len(_OUTS)))
    return got[0]
```
